# Optimizing a Trainium2 kernel written in Bass

```python
import numpy as np
import jax
import jax.numpy as jnp

def _softmax(x, axis=-1):
    return jax.nn.softmax(x, axis=axis)
def _gelu(x):
    return jax.nn.gelu(x, approximate=True)
def _silu(x):
    return jax.nn.silu(x)
def _sigmoid(x):
    return jax.nn.sigmoid(x)
def _layernorm(x, axis=-1, eps=1e-5):
    m = jnp.mean(x, axis=axis, keepdims=True)
    v = jnp.var(x, axis=axis, keepdims=True)
    return (x - m) / jnp.sqrt(v + eps)
def _scatter_add(tgt, idx, src, axis=0):
    return tgt.at[idx].add(src)
def _segment_sum(src, seg, n):
    return jax.ops.segment_sum(src, seg, n)

kernel_name = 'mk_conv_preact_d2_conv_nhwc192_5eef48'

def setup_inputs(seed: int = 0):
    np.random.seed(seed)
    _w = jnp.asarray
    def _rec_inputs():
        import jax
        import jax.numpy as jnp
        _gk = jax.random.key(seed)
        x = -0.001003 + 1 * jax.random.normal(jax.random.fold_in(_gk, 1), (8, 32, 32, 192), jnp.float32)
        return x
    x = _rec_inputs()
    def _L0_conv_setup():
        import jax, jax.numpy as jnp
        import numpy as np
        import math
        B_, H_, W_, DM = (8, 32, 32, 192)
        EXP = 2
        DI = EXP * DM
        N = 16
        K = 8
        R = math.ceil(DM / 16)

        def _scan_perm(size):
            idx = np.arange(size * size).reshape(size, size).copy()
            idx[1::2] = idx[1::2, ::-1]
            locs = idx.reshape(-1)
            return (jnp.asarray(locs), jnp.asarray(np.argsort(locs)))

        def _selective_scan(u, delta, A, Bs, Cs, D):
            uL = jnp.moveaxis(u, -1, 0)
            dL = jnp.moveaxis(delta, -1, 0)
            BL = jnp.moveaxis(Bs, -1, 0)
            CL = jnp.moveaxis(Cs, -1, 0)
            h0 = jnp.zeros(u.shape[:3] + (A.shape[-1],), u.dtype)

            def step(h, inp):
                ul, dl, bl, cl = inp
                dA = jnp.exp(dl[..., None] * A)
                h = dA * h + (dl * ul)[..., None] * bl[:, :, None, :]
                y = jnp.einsum('bkdn,bkn->bkd', h, cl)
                return (h, y)
            _, ys = jax.lax.scan(step, h0, (uL, dL, BL, CL))
            y = jnp.moveaxis(ys, 0, -1)
            return y + D[None, :, :, None] * u
        key = jax.random.key(seed)
        ks = jax.random.split(key, 8)
        x = jax.random.normal(ks[0], (B_, H_, W_, DM), jnp.float32)
        W_in = jax.random.normal(ks[1], (2 * DI, DM), jnp.float32) * DM ** (-0.5)
        conv_w = jax.random.normal(ks[2], (DI, 1, 3, 3), jnp.float32) * (1.0 / 3.0)
        conv_b = jnp.zeros((DI,), jnp.float32)
        x_proj_weight = jax.random.normal(ks[3], (K, R + 2 * N, DI), jnp.float32) * DI ** (-0.5)
        dt_std = R ** (-0.5)
        dt_projs_weight = jax.random.uniform(ks[4], (K, DI, R), jnp.float32, -dt_std, dt_std)
        dt = jnp.exp(jax.random.uniform(ks[5], (K, DI), jnp.float32) * (math.log(0.1) - math.log(0.001)) + math.log(0.001))
        dt = jnp.clip(dt, 0.0001)
        dt_projs_bias = dt + jnp.log(-jnp.expm1(-dt))
        A_logs = jnp.log(jnp.tile(jnp.arange(1, N + 1, dtype=jnp.float32)[None, :], (K * DI, 1)))
        Ds = jnp.ones((K * DI,), jnp.float32)
        ln_w = jnp.ones((DI,), jnp.float32)
        ln_b = jnp.zeros((DI,), jnp.float32)
        W_out = jax.random.normal(ks[6], (DM, DI), jnp.float32) * DI ** (-0.5)
        return dict(x=x, W_in=W_in, conv_w=conv_w, conv_b=conv_b, x_proj_weight=x_proj_weight, dt_projs_weight=dt_projs_weight, dt_projs_bias=dt_projs_bias, A_logs=A_logs, Ds=Ds, ln_w=ln_w, ln_b=ln_b, W_out=W_out)
    _L0_conv_all = _L0_conv_setup()
    _L0_conv_in = {k: v for k, v in _L0_conv_all.items() if k in ('W_in', 'conv_w', 'conv_b', 'x_proj_weight', 'dt_projs_weight', 'dt_projs_bias', 'A_logs', 'Ds', 'ln_w', 'ln_b', 'W_out', )}
    del _L0_conv_all

    def _L1_conv_setup():
        import jax, jax.numpy as jnp
        import numpy as np
        D_MODEL = 192
        D_STATE = 16
        D_CONV = 3
        EXPAND = 2
        D_INNER = EXPAND * D_MODEL
        DT_RANK = (D_MODEL + 15) // 16

        def _ssm_scan(u, W_x, W_dt, b_dt, A_log, D_param):
            x_dbl = u @ W_x
            dt = x_dbl[..., :DT_RANK]
            B_mat = x_dbl[..., DT_RANK:DT_RANK + D_STATE]
            C_mat = x_dbl[..., DT_RANK + D_STATE:]
            dt = jax.nn.softplus(dt @ W_dt + b_dt)
            A = -jnp.exp(A_log)
            log_dA = jnp.einsum('bld,dn->bldn', dt, A)
            dB_u = jnp.einsum('bld,bln->bldn', dt, B_mat) * u[..., None]
            log_decay = jnp.cumsum(log_dA, axis=1)
            decay = jnp.exp(log_decay)
            h = decay * jnp.cumsum(dB_u / (decay + 1e-12), axis=1)
            y = jnp.einsum('bldn,bln->bld', h, C_mat)
            return y + u * D_param
        key = jax.random.key(seed)
        ks = jax.random.split(key, 8)
        B, H, W = (4, 32, 32)
        sc = lambda n: 1.0 / np.sqrt(n)
        x = jax.random.normal(ks[0], (B, H, W, D_MODEL), jnp.float32)
        W_in = jax.random.normal(ks[1], (D_MODEL, 2 * D_INNER), jnp.float32) * sc(D_MODEL)
        conv_w = jax.random.normal(ks[2], (D_INNER, 1, D_CONV, D_CONV), jnp.float32) * sc(D_CONV * D_CONV)
        conv_b = jnp.zeros((D_INNER,), jnp.float32)
        W_x = jax.random.normal(ks[3], (D_INNER, DT_RANK + 2 * D_STATE), jnp.float32) * sc(D_INNER)
        W_dt = jax.random.normal(ks[4], (DT_RANK, D_INNER), jnp.float32) * sc(DT_RANK)
        b_dt = jnp.zeros((D_INNER,), jnp.float32)
        A_log = jnp.log(jnp.tile(jnp.arange(1, D_STATE + 1, dtype=jnp.float32), (D_INNER, 1)))
        D_param = jnp.ones((D_INNER,), jnp.float32)
        W_out = jax.random.normal(ks[5], (D_INNER, D_MODEL), jnp.float32) * sc(D_INNER)
        gamma = jnp.ones((D_INNER,), jnp.float32)
        beta = jnp.zeros((D_INNER,), jnp.float32)
        return {'x': x, 'W_in': W_in, 'conv_w': conv_w, 'conv_b': conv_b, 'W_x': W_x, 'W_dt': W_dt, 'b_dt': b_dt, 'A_log': A_log, 'D_param': D_param, 'W_out': W_out, 'gamma': gamma, 'beta': beta}
    _L1_conv_all = _L1_conv_setup()
    _L1_conv_in = {k: v for k, v in _L1_conv_all.items() if k in ('W_in', 'conv_w', 'conv_b', 'W_x', 'W_dt', 'b_dt', 'A_log', 'D_param', 'W_out', 'gamma', 'beta', )}
    del _L1_conv_all

    return {
        "x": x,
        "L0_conv_W_in": _L0_conv_in["W_in"],
        "L0_conv_conv_w": _L0_conv_in["conv_w"],
        "L0_conv_conv_b": _L0_conv_in["conv_b"],
        "L0_conv_x_proj_weight": _L0_conv_in["x_proj_weight"],
        "L0_conv_dt_projs_weight": _L0_conv_in["dt_projs_weight"],
        "L0_conv_dt_projs_bias": _L0_conv_in["dt_projs_bias"],
        "L0_conv_A_logs": _L0_conv_in["A_logs"],
        "L0_conv_Ds": _L0_conv_in["Ds"],
        "L0_conv_ln_w": _L0_conv_in["ln_w"],
        "L0_conv_ln_b": _L0_conv_in["ln_b"],
        "L0_conv_W_out": _L0_conv_in["W_out"],
        "L1_conv_W_in": _L1_conv_in["W_in"],
        "L1_conv_conv_w": _L1_conv_in["conv_w"],
        "L1_conv_conv_b": _L1_conv_in["conv_b"],
        "L1_conv_W_x": _L1_conv_in["W_x"],
        "L1_conv_W_dt": _L1_conv_in["W_dt"],
        "L1_conv_b_dt": _L1_conv_in["b_dt"],
        "L1_conv_A_log": _L1_conv_in["A_log"],
        "L1_conv_D_param": _L1_conv_in["D_param"],
        "L1_conv_W_out": _L1_conv_in["W_out"],
        "L1_conv_gamma": _L1_conv_in["gamma"],
        "L1_conv_beta": _L1_conv_in["beta"],
    }

def reference(x, L0_conv_W_in, L0_conv_conv_w, L0_conv_conv_b, L0_conv_x_proj_weight, L0_conv_dt_projs_weight, L0_conv_dt_projs_bias, L0_conv_A_logs, L0_conv_Ds, L0_conv_ln_w, L0_conv_ln_b, L0_conv_W_out, L1_conv_W_in, L1_conv_conv_w, L1_conv_conv_b, L1_conv_W_x, L1_conv_W_dt, L1_conv_b_dt, L1_conv_A_log, L1_conv_D_param, L1_conv_W_out, L1_conv_gamma, L1_conv_beta):
    import jax
    import jax.numpy as jnp
    def _L0_conv_ref(x, W_in, conv_w, conv_b, x_proj_weight, dt_projs_weight, dt_projs_bias, A_logs, Ds, ln_w, ln_b, W_out):
        import jax, jax.numpy as jnp
        import numpy as np
        import math
        B_, H_, W_, DM = (8, 32, 32, 192)
        EXP = 2
        DI = EXP * DM
        N = 16
        K = 8
        R = math.ceil(DM / 16)

        def _scan_perm(size):
            idx = np.arange(size * size).reshape(size, size).copy()
            idx[1::2] = idx[1::2, ::-1]
            locs = idx.reshape(-1)
            return (jnp.asarray(locs), jnp.asarray(np.argsort(locs)))

        def _selective_scan(u, delta, A, Bs, Cs, D):
            uL = jnp.moveaxis(u, -1, 0)
            dL = jnp.moveaxis(delta, -1, 0)
            BL = jnp.moveaxis(Bs, -1, 0)
            CL = jnp.moveaxis(Cs, -1, 0)
            h0 = jnp.zeros(u.shape[:3] + (A.shape[-1],), u.dtype)

            def step(h, inp):
                ul, dl, bl, cl = inp
                dA = jnp.exp(dl[..., None] * A)
                h = dA * h + (dl * ul)[..., None] * bl[:, :, None, :]
                y = jnp.einsum('bkdn,bkn->bkd', h, cl)
                return (h, y)
            _, ys = jax.lax.scan(step, h0, (uL, dL, BL, CL))
            y = jnp.moveaxis(ys, 0, -1)
            return y + D[None, :, :, None] * u
        B, H, W, C = x.shape
        L = H * W
        locs, locs_inv = _scan_perm(H)
        enc = lambda t: t[..., locs]
        dec = lambda t: t[..., locs_inv]
        xz = x @ W_in.T
        xc, z = jnp.split(xz, 2, axis=-1)
        xc = jnp.transpose(xc, (0, 3, 1, 2))
        xc = jax.lax.conv_general_dilated(xc, conv_w, (1, 1), 'SAME', feature_group_count=DI, dimension_numbers=('NCHW', 'OIHW', 'NCHW')) + conv_b[None, :, None, None]
        xc = jax.nn.silu(xc)
        f0 = enc(xc.reshape(B, DI, L))
        f1 = enc(jnp.swapaxes(xc, 2, 3).reshape(B, DI, L))
        xr = jnp.rot90(xc, k=1, axes=(2, 3))
        f2 = enc(xr.reshape(B, DI, L))
        f3 = enc(jnp.swapaxes(xr, 2, 3).reshape(B, DI, L))
        xs4 = jnp.stack([f0, f1, f2, f3], axis=1)
        xs = jnp.concatenate([xs4, jnp.flip(xs4, -1)], axis=1)
        x_dbl = jnp.einsum('bkdl,kcd->bkcl', xs, x_proj_weight)
        dts, Bsx, Csx = jnp.split(x_dbl, [R, R + N], axis=2)
        dts = jnp.einsum('bkrl,kdr->bkdl', dts, dt_projs_weight)
        delta = jax.nn.softplus(dts + dt_projs_bias[None, :, :, None])
        A = -jnp.exp(A_logs).reshape(K, DI, N)
        out_y = _selective_scan(xs, delta, A, Bsx, Csx, Ds.reshape(K, DI))
        inv_y = jnp.flip(out_y[:, K // 2:K], -1)
        y0 = dec(out_y[:, 0])
        y1 = dec(inv_y[:, 0])
        y2 = jnp.swapaxes(dec(out_y[:, 1]).reshape(B, DI, W, H), 2, 3).reshape(B, DI, L)
        y3 = jnp.swapaxes(dec(inv_y[:, 1]).reshape(B, DI, W, H), 2, 3).reshape(B, DI, L)
        y4 = jnp.rot90(dec(out_y[:, 2]).reshape(B, DI, W, H), k=3, axes=(2, 3)).reshape(B, DI, L)
        y5 = jnp.rot90(dec(inv_y[:, 2]).reshape(B, DI, W, H), k=3, axes=(2, 3)).reshape(B, DI, L)
        y6 = jnp.rot90(jnp.swapaxes(dec(out_y[:, 3]).reshape(B, DI, W, H), 2, 3), k=3, axes=(2, 3)).reshape(B, DI, L)
        y7 = jnp.rot90(jnp.swapaxes(dec(inv_y[:, 3]).reshape(B, DI, W, H), 2, 3), k=3, axes=(2, 3)).reshape(B, DI, L)
        y = y0 + y1 + y2 + y3 + y4 + y5 + y6 + y7
        y = jnp.swapaxes(y, 1, 2).reshape(B, H, W, DI)
        mu = jnp.mean(y, axis=-1, keepdims=True)
        var = jnp.var(y, axis=-1, keepdims=True)
        y = (y - mu) * jax.lax.rsqrt(var + 1e-05) * ln_w + ln_b
        y = y * jax.nn.silu(z)
        return y @ W_out.T

    def _L1_conv_ref(x, W_in, conv_w, conv_b, W_x, W_dt, b_dt, A_log, D_param, W_out, gamma, beta):
        import jax, jax.numpy as jnp
        import numpy as np
        D_MODEL = 192
        D_STATE = 16
        D_CONV = 3
        EXPAND = 2
        D_INNER = EXPAND * D_MODEL
        DT_RANK = (D_MODEL + 15) // 16

        def _ssm_scan(u, W_x, W_dt, b_dt, A_log, D_param):
            x_dbl = u @ W_x
            dt = x_dbl[..., :DT_RANK]
            B_mat = x_dbl[..., DT_RANK:DT_RANK + D_STATE]
            C_mat = x_dbl[..., DT_RANK + D_STATE:]
            dt = jax.nn.softplus(dt @ W_dt + b_dt)
            A = -jnp.exp(A_log)
            log_dA = jnp.einsum('bld,dn->bldn', dt, A)
            dB_u = jnp.einsum('bld,bln->bldn', dt, B_mat) * u[..., None]
            log_decay = jnp.cumsum(log_dA, axis=1)
            decay = jnp.exp(log_decay)
            h = decay * jnp.cumsum(dB_u / (decay + 1e-12), axis=1)
            y = jnp.einsum('bldn,bln->bld', h, C_mat)
            return y + u * D_param
        B, H, W, C = x.shape
        xz = x @ W_in
        x_val, z = (xz[..., :D_INNER], xz[..., D_INNER:])
        xc = jnp.transpose(x_val, (0, 3, 1, 2))
        xc = jax.lax.conv_general_dilated(xc, conv_w, window_strides=(1, 1), padding='SAME', feature_group_count=D_INNER, dimension_numbers=('NCHW', 'OIHW', 'NCHW'))
        xc = xc + conv_b[None, :, None, None]
        xc = jax.nn.silu(xc)
        xv = jnp.transpose(xc, (0, 2, 3, 1))
        scan = lambda u: _ssm_scan(u, W_x, W_dt, b_dt, A_log, D_param)
        s1 = xv.reshape(B, H * W, D_INNER)
        s2 = s1[:, ::-1]
        s3 = jnp.transpose(xv, (0, 2, 1, 3)).reshape(B, W * H, D_INNER)
        s4 = s3[:, ::-1]
        y1 = scan(s1)
        y2 = scan(s2)[:, ::-1]
        y3 = scan(s3)
        y4 = scan(s4)[:, ::-1]
        y3 = jnp.transpose(y3.reshape(B, W, H, D_INNER), (0, 2, 1, 3)).reshape(B, H * W, D_INNER)
        y4 = jnp.transpose(y4.reshape(B, W, H, D_INNER), (0, 2, 1, 3)).reshape(B, H * W, D_INNER)
        y = y1 + y2 + y3 + y4
        mu = jnp.mean(y, axis=-1, keepdims=True)
        var = jnp.mean(jnp.square(y - mu), axis=-1, keepdims=True)
        y = (y - mu) * jax.lax.rsqrt(var + 1e-05) * gamma + beta
        y = y.reshape(B, H, W, D_INNER) * jax.nn.silu(z)
        return y @ W_out

    def _gn(v, G=32, eps=1e-5):
        B_, H_, W_, C_ = v.shape
        g = v.reshape(B_, H_, W_, G, C_ // G)
        m = jnp.mean(g, axis=(1, 2, 4), keepdims=True)
        s = jnp.var(g, axis=(1, 2, 4), keepdims=True)
        return ((g - m) / jnp.sqrt(s + eps)).reshape(v.shape)

    def _ln_c(v, eps=1e-6):
        m = jnp.mean(v, axis=-1, keepdims=True)
        s = jnp.var(v, axis=-1, keepdims=True)
        return (v - m) / jnp.sqrt(s + eps)

    def _ln_t(v, eps=1e-5):
        m = jnp.mean(v, axis=-1, keepdims=True)
        s = jnp.var(v, axis=-1, keepdims=True)
        return (v - m) / jnp.sqrt(s + eps)

    def _to_tokens(v):
        B_, H_, W_, C_ = v.shape
        return v.reshape(B_, H_ * W_, C_)
    def _from_tokens(t, like):
        return t.reshape(like.shape)

    x = x + _L0_conv_ref(_gn(x), L0_conv_W_in, L0_conv_conv_w, L0_conv_conv_b, L0_conv_x_proj_weight, L0_conv_dt_projs_weight, L0_conv_dt_projs_bias, L0_conv_A_logs, L0_conv_Ds, L0_conv_ln_w, L0_conv_ln_b, L0_conv_W_out)
    x = x + _L1_conv_ref(_gn(x), L1_conv_W_in, L1_conv_conv_w, L1_conv_conv_b, L1_conv_W_x, L1_conv_W_dt, L1_conv_b_dt, L1_conv_A_log, L1_conv_D_param, L1_conv_W_out, L1_conv_gamma, L1_conv_beta)
    return x


_drawn_inputs = setup_inputs


def setup_inputs(seed=0):
    import zlib

    import numpy as np

    out = dict(_drawn_inputs(seed))
    spreads = {'L0_conv_conv_b': (0.0, 0.1),
     'L0_conv_Ds': (1.0, 0.6),
     'L0_conv_ln_w': (1.0, 0.2),
     'L0_conv_ln_b': (0.0, 0.1),
     'L1_conv_conv_b': (0.0, 0.1),
     'L1_conv_b_dt': (0.0, 0.8),
     'L1_conv_D_param': (1.0, 0.2),
     'L1_conv_gamma': (1.0, 0.2),
     'L1_conv_beta': (0.0, 0.1)}
    factors = {'L0_conv_x_proj_weight': 2.946,
     'L0_conv_dt_projs_weight': 8.0,
     'L0_conv_dt_projs_bias': 4.314,
     'L0_conv_A_logs': 7.025,
     'L1_conv_W_x': 5.713,
     'L1_conv_W_dt': 8.0,
     'L1_conv_A_log': 8.0}
    for name, (base, spread) in spreads.items():
        noise = np.random.default_rng([zlib.crc32(name.encode()), seed]).standard_normal(out[name].shape)
        drawn = base * np.exp(spread * noise) if base else spread * noise
        out[name] = jnp.asarray(drawn.astype(out[name].dtype))
    for name, factor in factors.items():
        out[name] = (out[name] * factor).astype(out[name].dtype)
    return out
```

```python
import concourse.bass as bass
from concourse import mybir
from contextlib import ExitStack

F32 = mybir.dt.float32
BF16 = mybir.dt.bfloat16
ALU = mybir.AluOpType
ACT = mybir.ActivationFunctionType

P = 128
NB, SIDE, C, DI, N, R, K = 8, 32, 192, 384, 16, 12, 8
T = SIDE * SIDE
HT = T // 2
CH = C // 2
J = DI // P
XR = 6 * N
PAD = SIDE + 2
PAIRS = N // 2
Q = 4

SCANS = [(0, "rows", False), (4, "rows", True), (3, "mirror", False), (7, "mirror", True),
         (1, "cols", False), (5, "cols", True), (2, "cols", True), (6, "cols", False)]
PIECES = [(0, 1), (1, 3), (3, 5), (5, 7), (7, 8)]
LN_1E12 = 27.631021115928547


def opens(i):
    return i == 0 or SCANS[i][1] != SCANS[i - 1][1]


def closes(i):
    return i == K - 1 or SCANS[i][1] != SCANS[i + 1][1]


def lines(ap, order):
    if order == "cols":
        v = ap.rearrange("p (r i two) -> p two i r", r=SIDE, two=2)
    else:
        v = ap.rearrange("p (i two c) -> p two i c", two=2, c=SIDE)
    if order == "mirror":
        return v[:, 0, :, ::-1], v[:, 1, :, :]
    return v[:, 0, :, :], v[:, 1, :, ::-1]


def stored(ap):
    v = ap.rearrange("p (i two c) -> p two i c", two=2, c=SIDE)
    return v[:, 0, :, :], v[:, 1, :, :]


class Counts:

    def __init__(self, known=None):
        self.known, self.now, self.marks = known, {}, {}

    def note(self, kind, step, by=1):
        self.now[kind] = self.now.get(kind, 0) + by
        self.marks[kind, step] = self.now[kind]
        return by

    def at(self, kind, step, b):
        if self.known is None:
            return 1
        return b * self.known.now[kind] + self.known.marks[kind, step]


def program(nc, counts, x, out, w_in, conv_w, conv_b, w_x0, w_dt0, dt_b0, a_log0, d0,
            w_x1, w_dt1, dt_b1, a_log1, d1, ln_w, ln_b, w_out, group_mean, eye, pick, mean_one):
    ctx = ExitStack()
    with ctx:
        def sb(name, shape, dt=F32):
            return ctx.enter_context(nc.sbuf_tensor(name, shape, dt))

        def semaphore(name):
            return ctx.enter_context(nc.semaphore(name))

        identity = sb("identity", [P, P])
        mean_ones = sb("mean_ones", [P, P])
        groups = sb("groups", [CH, CH])
        pick_f = sb("pick_f", [XR, 2 * N])
        pick_row = sb("pick_row", [XR, 2 * N], BF16)
        one = sb("one", [P, 1])
        eps = sb("eps", [P, 1])
        guard = sb("guard", [P, 1])
        win = sb("win", [CH, 2, 2, 2 * DI])
        cw = sb("cw", [P, 2, J, 9])
        cb = sb("cb", [P, 2, J])
        wx = sb("wx", [P, 2, J, XR + R])
        wdt = sb("wdt", [XR + R, 2, DI])
        wx1 = sb("wx1", [P, J, XR + R])
        wdt1 = sb("wdt1", [XR + R, DI])
        dtb0 = sb("dtb0", [P, K, J])
        dtb1 = sb("dtb1", [P, J])
        a0 = sb("a0", [P, K * J * N])
        a1 = sb("a1", [P, J * N])
        a1_now = sb("a1_now", [P, 2])
        dk = sb("dk", [P, J, K])
        skip = sb("skip", [P, 2, J])
        lnw = sb("lnw", [P, 2, J])
        lnb = sb("lnb", [P, 2, J])
        wout = sb("wout", [P, 2, J, C])
        xT = sb("xT", [CH, 2, T])
        gate = sb("gate", [P, J, T])
        u = sb("u", [P, J, T])
        y = sb("y", [P, J, T])
        B_all = sb("B_all", [P, 2, T])
        C_all = sb("C_all", [P, 2, T])
        parts = sb("parts", [XR, 2, T], BF16)
        xdbl = sb("xdbl", [XR + R, T])
        stats = sb("stats", [CH, 2, 2, 6])
        mv = sb("mv", [CH, 2, 2])
        sq2 = sb("sq2", [CH, 2])
        gs = sb("gs", [CH, 2, 2])
        gvar = sb("gvar", [CH, 2])
        rstd = sb("rstd", [CH, 2])
        room = sb("room", [P, 26, T])
        ordered = room[:, 0:3, :]
        delta0 = room[:, 3:9, :].rearrange("p (s j) t -> p s j t", s=2)
        du0 = room[:, 9:15, :].rearrange("p (s j) t -> p s j t", s=2)
        decay0 = room[:, 17:20, :]
        state0 = room[:, 20:26, :].rearrange("p (s j) t -> p s j t", s=2)
        delta1 = room[:, 0:3, :]
        du1 = room[:, 3:6, :]
        csum = room[:, 6:10, :]
        decay1 = room[:, 10:14, :].rearrange("p (s o) t -> p s o t", s=2)
        src1 = room[:, 14:16, :]
        state1 = room[:, 16:24, :].rearrange("p (s q) t -> p s q t", s=2)
        yc1 = room[:, 24:26, :]
        delta_cols = room[:, 24, :]
        soft = [room[:, 15:17, :], room[:, 14:16, :]]
        xn = room[0:CH, 17:19, :]
        padded = room[:, 20:24, :].rearrange("p a t -> p (a t)")[:, 0:J * PAD * PAD].rearrange(
            "p (j r c) -> p j r c", j=J, r=PAD)
        mu = room[:, 20, :]
        rs = room[:, 21, :]
        sq = room[:, 22:25, :]
        o2 = room[0:CH, 17:19, :]

        bank = ctx.enter_context(nc.psum_tensor("bank", [P, 8, HT], F32))
        WORK = (6, 7)
        yacc0 = bank[:, 0:6, :].rearrange("p (j h) t -> p j h t", j=J)
        yacc1 = bank[:, 0:2, :]
        hsum = bank[:, 2:6, :].rearrange("p (s h) t -> p s h t", s=2)

        names = ["load_wx0", "load_wx1", "mm", "ev", "stat", "gs", "xn", "pad", "conv", "u",
                 "uo", "p1", "r1", "p2", "parts", "ab", "ex", "ln", "w1", "q", "g", "dl", "du",
                 "yinit", "yev", "cs", "dc", "cen", "sq", "lnv", "rs", "nrm", "aff", "gat", "res"]
        S = {n: semaphore("s_" + n) for n in names}
        note, at = counts.note, counts.at
        setup = semaphore("setup")
        loaded = semaphore("loaded")
        exp_a = semaphore("exp_a")
        load_x_done = semaphore("load_x_done")
        store_done = semaphore("store_done")
        decay_ready = [semaphore(f"decay_ready_tile{j}") for j in range(J)]
        source_ready = [semaphore(f"source_ready_tile{j}") for j in range(J)]
        scanned = [semaphore(f"scanned_tile{j}") for j in range(J)]
        weighted = [semaphore(f"weighted_tile{j}") for j in range(J)]
        summed = [semaphore(f"summed_tile{j}") for j in range(J)]
        B_spread = semaphore("B_spread")
        C_spread = semaphore("C_spread")
        B_ready = semaphore("B_ready")
        C_ready = semaphore("C_ready")
        a1_ready = semaphore("a1_ready")
        decay1_ready = semaphore("decay1_ready")
        gate1_ready = semaphore("gate1_ready")
        src1_ready = semaphore("src1_ready")
        pool1_ready = semaphore("pool1_ready")
        dve1_ready = semaphore("dve1_ready")
        scanned1 = semaphore("scanned1")
        hsum_ready = semaphore("hsum_ready")
        weighted1 = semaphore("weighted1")
        summed1 = semaphore("summed1")
        NB_SPREAD = K * N + J * N

        def halves(h):
            return slice(h * HT, (h + 1) * HT)

        block = ctx.enter_context(nc.Block())
        LOADS = 20

        @block.sync
        def _(sp):
            def load(dst, src):
                sp.dma_start(dst, src).then_inc(loaded, 16)

            load(groups[:, :], group_mean)
            load(identity[:, :], eye)
            load(pick_f[:, :], pick)
            load(dtb0[:, :, :], dt_b0)
            load(dtb1[:, :], dt_b1)
            load(a0[:, :], a_log0)
            load(a1[:, :], a_log1)
            load(dk[:, :, :], d0)
            load(skip[:, 1, :], d1)
            for l in range(2):
                load(win[:, l, :, :], w_in[l].rearrange("(h p) m -> p h m", p=CH))
                load(wout[:, l, :, :], w_out[l].rearrange("(j p) c -> p j c", p=P))
            load(cw[:, :, :, :], conv_w)
            load(cb[:, :, :], conv_b)
            load(lnw[:, :, :], ln_w)
            load(lnb[:, :, :], ln_b)
            load(wx1[:, :, :], w_x1)
            load(wdt1[XR:XR + R, :], w_dt1)
            load(mean_ones[:, :], mean_one)
            def load_x(b):
                src = x[slice(b, b + 1) if isinstance(b, int) else bass.ds(b, 1), :, :]
                sp.dma_start(xT[:, :, :], src.rearrange("o (h p) t -> p (o h) t", p=CH)).then_inc(load_x_done, 16)

            def image(b):
                for i, (k, _, _) in enumerate(SCANS):
                    if i >= 2:
                        sp.wait_ge(S["ev"], at("ev", ("dt", 0, i - 2, J - 1, 1), b))
                    slot = f"load_wx{i % 2}"
                    sp.dma_start(wx[:, i % 2, :, :], w_x0[k]).then_inc(S[slot], note(slot, i, 16))
                    sp.dma_start(wdt[XR:XR + R, i % 2, :], w_dt0[k]).then_inc(S[slot], note(slot, i, 16))
                sp.wait_ge(S["res"], at("res", (1, 1), b))
                dst = out[slice(b, b + 1) if isinstance(b, int) else bass.ds(b, 1), :, :]
                sp.dma_start(dst.rearrange("o (h p) t -> p (o h) t", p=CH), xT[:, :, :]).then_inc(store_done, 16)
                sp.wait_ge(store_done, b * 16 + 16)

            load_x(0)
            before = dict(counts.now)
            if NB > 1:
                with sp.Fori(0, NB - 1) as b:
                    image(b)
                    load_x(b + 1)
            counts.now = before
            image(NB - 1)

        @block.tensor
        def _(pe):
            last = {}

            def work(b, h, step, waits, products, rows=P, cols=HT):
                free = last[h](b) if last[h] else None
                if free:
                    pe.wait_ge(*free)
                for kind, s in waits:
                    if free and S[kind] is free[0]:
                        continue
                    pe.wait_ge(S[kind], at(kind, s, b))
                for i, (lhsT, rhs) in enumerate(products):
                    ins = nc.tensor.matmul(bank[0:rows, WORK[h], 0:cols], lhsT, rhs,
                                           start=(i == 0), stop=(i == len(products) - 1))
                ins.then_inc(S["mm"], note("mm", step))
                last[h] = lambda b, step=step: (S["ev"], at("ev", step, b))

            def front(b, l):
                work(b, 0, ("gn", l), [("stat", (l, "msq"))],
                     [(groups[:, :], mv[:, :, :].rearrange("p h s -> p (h s)"))], rows=CH, cols=4)
                for m in range(2 * J):
                    for h in range(2):
                        work(b, h, ("in", l, m, h), [("xn", (l, 1))],
                             [(win[:, l, c, m * P:(m + 1) * P], xn[:, c, halves(h)]) for c in range(2)])

            def prepare_bc(b, l, i):
                src = ordered if l == 0 else u
                w = wx[:, i % 2, :, :] if l == 0 else wx1
                waits = [("uo", max(o for o in range(i + 1) if opens(o))), (f"load_wx{i % 2}", i)] if l == 0 else [("u", (1, J - 1))]
                for h in range(2):
                    work(b, h, ("xd", l, i, h), waits,
                         [(w[:, j, :], src[:, j, halves(h)]) for j in range(J)], rows=XR + R)

            def prepare_dt(b, l, i, j):
                w = wdt[XR:XR + R, i % 2, :] if l == 0 else wdt1[XR:XR + R, :]
                for h in range(2):
                    work(b, h, ("dt", l, i, j, h), [("ev", ("xd", l, i, h))],
                         [(w[:, j * P:(j + 1) * P], xdbl[XR:XR + R, halves(h)])])

            def spread(b, row, par, h, sem):
                nc.tensor.matmul(bank[:, WORK[h], :], pick_row[:, row].broadcast_to([XR, P]),
                                 parts[:, par, halves(h)], start=True, stop=True).then_inc(sem, 1)

            def add_state(b, G, j, p, start, stop, par):
                for h in range(2):
                    ins = nc.tensor.matmul(yacc0[:, j, h, :], identity[:, :], state0[:, p, j, halves(h)],
                                           start=start, stop=stop)
                ins.then_inc(summed[j], 1)

            def pair0(b, i, it, first, end, prepared=None):
                for p in range(2):
                    G = b * (K * N) + i * N + it * 2 + p
                    GS = b * NB_SPREAD + i * N + it * 2 + p
                    n = it * 2 + p
                    if prepared and p == 0:
                        pe.wait_ge(S["ev"], at("ev", (*prepared, 1), b))
                    new_scan = end and p == 1
                    if not (new_scan and i == K - 1):
                        par, row = (i % 2, n + 1) if not new_scan else ((i + 1) % 2, 0)
                        sel = slice(row, row + 1) if isinstance(row, int) else bass.ds(row, 1)
                        selC = slice(row + N, row + N + 1) if isinstance(row, int) else bass.ds(row + N, 1)
                        if new_scan:
                            pe.wait_ge(S["parts"], at("parts", (0, i + 1), b))
                        for h in range(2):
                            pe.wait_ge(C_ready, GS * 2 + (h + 1))
                            spread(b, sel, par, h, B_spread)
                        for h in range(2):
                            pe.wait_ge(B_ready, GS * 2 + (h + 3))
                            spread(b, selC, par, h, C_spread)
                    start = first and p == 0 and opens(i)
                    for j in range(J):
                        if start and i > 0:
                            pe.wait_ge(S["yev"], at("yev", (0, i - 1, j), b))
                        pe.wait_ge(weighted[j], G + 1)
                        add_state(b, G, j, p, start, end and p == 1 and closes(i), i % 2)

            def scans0(b):
                prepare_bc(b, 0, 0)
                for j in range(J):
                    prepare_dt(b, 0, 0, j)
                pe.wait_ge(S["parts"], at("parts", (0, 0), b))
                GS = b * NB_SPREAD
                for h in range(2):
                    pe.wait_ge(*last[h](b))
                    spread(b, slice(0, 1), 0, h, B_spread)
                for h in range(2):
                    pe.wait_ge(B_ready, GS * 2 + (h + 1))
                    spread(b, slice(N, N + 1), 0, h, C_spread)
                for i in range(K):
                    for s, (lo, hi) in enumerate(PIECES):
                        prepared = None
                        if s > 0 and i < K - 1:
                            prepared = ("xd", 0, i + 1) if s == 1 else ("dt", 0, i + 1, s - 2)
                        if hi - lo == 1:
                            pair0(b, i, lo, lo == 0, hi == PAIRS, prepared)
                        else:
                            with pe.Fori(lo, hi) as it:
                                pair0(b, i, it, False, False, prepared)
                        if i < K - 1 and s < 4:
                            done = b * (NB_SPREAD * 2) + (i * N + 2 * hi) * 2
                            for h in range(2):
                                last[h] = lambda b, h=h, v=done: (C_ready, v + (h + 1))
                            if s == 0:
                                prepare_bc(b, 0, i + 1)
                            else:
                                prepare_dt(b, 0, i + 1, s - 1)

            def pair1(b, j, it, first, end):
                for p in range(2):
                    n = it * 2 + p
                    G = b * (J * N) + j * N + it * 2 + p
                    GS = b * NB_SPREAD + (K * N + j * N) + it * 2 + p
                    is0 = first and p == 0
                    is15 = end and p == 1
                    if not is15:
                        sel = slice(n + 1, n + 2) if isinstance(n, int) else bass.ds(n + 1, 1)
                        for h in range(2):
                            if not is0:
                                pe.wait_ge(C_ready, GS * 2 - (1 - h))
                            else:
                                pe.wait_ge(B_ready, GS * 2 + (h + 1))
                            spread(b, sel, 0, h, B_spread)
                    selC = slice(n + N, n + N + 1) if isinstance(n, int) else bass.ds(n + N, 1)
                    for h in range(2):
                        if not is15:
                            pe.wait_ge(B_ready, GS * 2 + (h + 3))
                        else:
                            pe.wait_ge(C_ready, GS * 2 - (1 - h))
                        spread(b, selC, 0, h, C_spread)
                    if not (first and j == 0):
                        pe.wait_ge(weighted1, G - 1)

                    def add_direction(q):
                        pe.wait_ge(scanned1, G * 4 + (q + 1))
                        for h in range(2):
                            if q < 2:
                                rhs = state1[:, p, q, halves(h)]
                            else:
                                rhs = state1[:, p, q, :].rearrange("p (c r) -> p r c", c=SIDE)[
                                    :, h * (SIDE // 2):(h + 1) * (SIDE // 2), :]
                            ins = nc.tensor.matmul(hsum[:, p, h, :], identity[:, :], rhs,
                                                   start=(q == 0), stop=(q == Q - 1))
                        ins.then_inc(hsum_ready, 1)

                    add_direction(0)
                    add_direction(1)
                    if not is0:
                        add_weighted(b, j, G, 1 - p, first and p == 1, False)
                    add_direction(2)
                    add_direction(3)

            def add_weighted(b, j, G, slot, start, stop):
                if start and j > 0:
                    pe.wait_ge(S["yev"], at("yev", (1, j - 1), b))
                pe.wait_ge(weighted1, G)
                for h in range(2):
                    ins = nc.tensor.matmul(yacc1[:, h, :], identity[:, :], yc1[:, slot, halves(h)],
                                           start=start, stop=stop)
                ins.then_inc(summed1, 1)

            def scans1(b):
                prepare_bc(b, 1, 0)
                for j in range(J):
                    prepare_dt(b, 1, 0, j)
                pe.wait_ge(S["parts"], at("parts", (1, 0), b))
                for j in range(J):
                    for h in range(2):
                        if j == 0:
                            pe.wait_ge(*last[h](b))
                        else:
                            pe.wait_ge(C_ready, b * (2 * NB_SPREAD) + (K * N + j * N) * 2 - (1 - h))
                        spread(b, slice(0, 1), 0, h, B_spread)
                    pair1(b, j, 0, True, False)
                    with pe.Fori(1, PAIRS - 1) as it:
                        pair1(b, j, it, False, False)
                    pair1(b, j, PAIRS - 1, False, True)
                    add_weighted(b, j, b * (J * N) + (j + 1) * N, 1, False, True)
                for h in range(2):
                    last[h] = lambda b, h=h: (C_ready, b * (2 * NB_SPREAD) + NB_SPREAD * 2 - (1 - h))

            def tail(b, l):
                yev = [("yev", (0, K - 1, J - 1) if l == 0 else (1, J - 1))]
                for h in range(2):
                    work(b, h, ("mu", l, h), yev, [(mean_ones[:, :], y[:, j, halves(h)]) for j in range(J)])
                for h in range(2):
                    work(b, h, ("var", l, h), [("sq", (l, J - 1))],
                         [(mean_ones[:, :], sq[:, j, halves(h)]) for j in range(J)])
                for c in range(2):
                    for h in range(2):
                        work(b, h, ("out", l, c, h), [("gat", (l, J - 1))],
                             [(wout[:, l, j, c * CH:(c + 1) * CH], y[:, j, halves(h)]) for j in range(J)],
                             rows=CH)

            pe.wait_ge(loaded, 16 * LOADS)
            pe.wait_ge(setup, 8)
            with pe.Fori(0, NB) as b:
                for h in range(2):
                    last[h] = None
                front(b, 0)
                scans0(b)
                for h in range(2):
                    last[h] = lambda b, h=h: (C_ready, b * (2 * NB_SPREAD) + 2 * K * N - (1 - h))
                tail(b, 0)
                front(b, 1)
                scans1(b)
                tail(b, 1)

        @block.scalar
        def _(act):
            def take(b, step, dst, h, func=ACT.Copy, rows=P, cols=HT, src=None, **kw):
                act.wait_ge(S["mm"], at("mm", step, b))
                nc.scalar.activation(dst, bank[0:rows, WORK[h], 0:cols] if src is None else src, func,
                                     **kw).then_inc(S["ev"], note("ev", step))

            def front(b, l):
                take(b, ("gn", l), gs[:, :, :].rearrange("p h s -> p (h s)"), 0, rows=CH, cols=4)
                act.wait_ge(S["stat"], at("stat", (l, "gvar"), b))
                nc.scalar.activation(rstd[:, :], gvar[:, :], ACT.Ln, bias=eps[0:CH, :]).then_inc(
                    S["gs"], note("gs", (l, "ln")))
                act.wait_ge(S["gs"], at("gs", (l, "ln"), b))
                nc.scalar.activation(rstd[:, :], rstd[:, :], ACT.Exp, scale=-0.5).then_inc(
                    S["gs"], note("gs", (l, "rstd")))
                act.wait_ge(S["pad"], at("pad", l, b))
                for m in range(2 * J):
                    for h in range(2):
                        if m < J:
                            rows = slice(1 + h * (SIDE // 2), 1 + (h + 1) * (SIDE // 2))
                            take(b, ("in", l, m, h), padded[:, m, rows, 1:1 + SIDE], h,
                                 src=bank[:, WORK[h], :].rearrange("p (r c) -> p r c", c=SIDE))
                        else:
                            take(b, ("in", l, m, h), gate[:, m - J, halves(h)], h, func=ACT.Silu)
                for j in range(J):
                    act.wait_ge(S["conv"], at("conv", (l, j, 8), b))
                    nc.scalar.activation(u[:, j, :], u[:, j, :], ACT.Silu).then_inc(S["u"], note("u", (l, j)))
                for j in range(J):
                    act.wait_ge(S["u"], at("u", (l, j), b))
                    nc.scalar.activation(y[:, j, :], u[:, j, :], ACT.Copy, scale=skip[:, l, j:j + 1]).then_inc(
                        S["yinit"], note("yinit", (l, j)))

            def reorder(b, i):
                if i > 0:
                    act.wait_ge(S["du"], at("du", (0, i - 1, J - 1), b))
                for j in range(J):
                    for src, dst in zip(lines(u[:, j, :], SCANS[i][1]), stored(ordered[:, j, :])):
                        nc.scalar.activation(dst, src, ACT.Copy).then_inc(S["uo"], note("uo", i))

            def prepare_bc(b, l, i):
                for h in range(2):
                    take(b, ("xd", l, i, h), xdbl[:, halves(h)], h, rows=XR + R)
                slot = parts[:, i % 2, :]
                act.wait_ge(S["ev"], at("ev", ("xd", l, i, 1), b))
                nc.scalar.activation(slot[:, :], xdbl[0:XR, :], ACT.Copy).then_inc(S["p1"], note("p1", (l, i)))
                act.wait_ge(S["r1"], at("r1", (l, i), b))
                nc.scalar.activation(slot[32:64, :], xdbl[32:64, :], ACT.Copy).then_inc(S["p2"], note("p2", (l, i, 0)))
                nc.scalar.activation(slot[64:96, :], xdbl[64:96, :], ACT.Copy).then_inc(S["p2"], note("p2", (l, i)))

            def prepare_dt(b, l, i, j):
                delta = delta0[:, i % 2, j, :] if l == 0 else delta1[:, j, :]
                e = du0[:, i % 2, j, :] if l == 0 else du1[:, j, :]
                bias = dtb0[:, SCANS[i][0], j:j + 1] if l == 0 else dtb1[:, j:j + 1]
                log_w, w = soft[l][:, 0, :], soft[l][:, 1, :]
                for h in range(2):
                    take(b, ("dt", l, i, j, h), delta[:, halves(h)], h, func=ACT.Identity, bias=bias)
                act.wait_ge(S["ev"], at("ev", ("dt", l, i, j, 1), b))
                nc.scalar.activation(e, delta, ACT.Abs).then_inc(S["ab"], note("ab", (l, i, j)))
                act.wait_ge(S["ab"], at("ab", (l, i, j), b))
                nc.scalar.activation(e, e, ACT.Exp, scale=-1.0).then_inc(S["ex"], note("ex", (l, i, j)))
                act.wait_ge(S["ex"], at("ex", (l, i, j), b))
                if j > 0:
                    act.wait_ge(S["dl"], at("dl", (l, i, j - 1), b))
                elif i > 0:
                    act.wait_ge(S["dl"], at("dl", (l, i - 1, J - 1), b))
                nc.scalar.activation(log_w, e, ACT.Ln, bias=one[:, :]).then_inc(S["ln"], note("ln", (l, i, j)))
                nc.scalar.activation(w, e, ACT.Identity, bias=one[:, :]).then_inc(S["w1"], note("w1", (l, i, j)))

            def take_spread(GS, h, slot, sem_in, sem_out, dst):
                act.wait_ge(sem_in, GS * 2 + (h + 1))
                nc.scalar.activation(dst[:, slot, halves(h)], bank[:, WORK[h], :], ACT.Copy).then_inc(sem_out, 1)

            def pair0(b, i, it, first, end):
                for p in range(2):
                    n = it * 2 + p
                    G = b * (K * N) + i * N + it * 2 + p
                    GS = b * NB_SPREAD + i * N + it * 2 + p
                    start = i == 0 and first and p == 0
                    for j in range(J):
                        if first and p == 0:
                            act.wait_ge(S["dl"], at("dl", (0, i, j), b))
                        if not start:
                            act.wait_ge(scanned[j], G)
                        col = (SCANS[i][0] * J + j) * N + n
                        sel = slice(col, col + 1) if isinstance(col, int) else bass.ds(col, 1)
                        nc.scalar.activation(decay0[:, j, :], delta0[:, i % 2, j, :], ACT.Exp,
                                             scale=a0[:, sel]).then_inc(decay_ready[j], 1)
                    if i == K - 1 and end and p == 1:
                        continue
                    if not start:
                        act.wait_ge(source_ready[J - 1], G)
                    for h in range(2):
                        take_spread(GS + 1, h, 1 - p, B_spread, B_ready, B_all)
                    if not start:
                        act.wait_ge(weighted[J - 1], G)
                    for h in range(2):
                        take_spread(GS + 1, h, 1 - p, C_spread, C_ready, C_all)

            def scans0(b):
                reorder(b, 0)
                prepare_bc(b, 0, 0)
                for j in range(J):
                    prepare_dt(b, 0, 0, j)
                GS = b * NB_SPREAD
                for h in range(2):
                    take_spread(GS, h, 0, B_spread, B_ready, B_all)
                for h in range(2):
                    take_spread(GS, h, 0, C_spread, C_ready, C_all)
                for i in range(K):
                    for s, (lo, hi) in enumerate(PIECES):
                        if hi - lo == 1:
                            pair0(b, i, lo, lo == 0, hi == PAIRS)
                        else:
                            with act.Fori(lo, hi) as it:
                                pair0(b, i, it, False, False)
                        if i < K - 1 and s < 4:
                            if s == 0:
                                if opens(i + 1):
                                    reorder(b, i + 1)
                                prepare_bc(b, 0, i + 1)
                            else:
                                prepare_dt(b, 0, i + 1, s - 1)

            def pair1(b, j, it, first, end):
                for p in range(2):
                    n = it * 2 + p
                    G = b * (J * N) + j * N + it * 2 + p
                    GS = b * NB_SPREAD + (K * N + j * N) + it * 2 + p
                    fresh = j == 0 and first
                    col = j * N + n
                    sel = slice(col, col + 1) if isinstance(col, int) else bass.ds(col, 1)
                    if not fresh:
                        act.wait_ge(gate1_ready, G * 4 - 4)
                    nc.scalar.activation(a1_now[:, p:p + 1], a1[:, sel], ACT.Copy).then_inc(a1_ready, 1)
                    act.wait_ge(a1_ready, G + 1)
                    for o in range(2):
                        if not fresh:
                            act.wait_ge(scanned1, G * 4 - (8 - 2 * (o + 1)))
                        src = delta1[:, j, :]
                        dst = decay1[:, p, o, :]
                        if o == 1:
                            src = src.rearrange("p (r c) -> p c r", r=SIDE)
                            dst = dst.rearrange("p (c r) -> p c r", c=SIDE)
                        nc.scalar.activation(dst, src, ACT.Exp, scale=a1_now[:, p:p + 1]).then_inc(decay1_ready, 1)
                    for q in range(Q):
                        if first and p == 0:
                            act.wait_ge(S["cs"], at("cs", (j, q), b))
                        if not fresh:
                            act.wait_ge(hsum_ready, G * 4 - (8 - (q + 1)))
                        nc.scalar.activation(state1[:, p, q, :], csum[:, q, :], ACT.Sigmoid,
                                             scale=a1_now[:, p:p + 1], bias=guard[:, :]).then_inc(gate1_ready, 1)
                    if not (end and p == 1):
                        if not (j == 0 and first and p == 0):
                            act.wait_ge(src1_ready, G)
                        for h in range(2):
                            take_spread(GS + 1, h, 1 - p, B_spread, B_ready, B_all)
                    if not (first and j == 0):
                        act.wait_ge(weighted1, G - 1)
                    for h in range(2):
                        take_spread(GS, h, p, C_spread, C_ready, C_all)

            def scans1(b):
                prepare_bc(b, 1, 0)
                for j in range(J):
                    prepare_dt(b, 1, 0, j)
                for j in range(J):
                    GS = b * NB_SPREAD + (K * N + j * N)
                    if j > 0:
                        act.wait_ge(src1_ready, b * (J * N) + j * N - 1)
                    for h in range(2):
                        take_spread(GS, h, 0, B_spread, B_ready, B_all)
                    pair1(b, j, 0, True, False)
                    with act.Fori(1, PAIRS - 1) as it:
                        pair1(b, j, it, False, False)
                    pair1(b, j, PAIRS - 1, False, True)

            def tail(b, l):
                for h in range(2):
                    take(b, ("mu", l, h), mu[:, halves(h)], h)
                for j in range(J):
                    act.wait_ge(S["cen"], at("cen", (l, j), b))
                    nc.scalar.activation(sq[:, j, :], y[:, j, :], ACT.Square).then_inc(S["sq"], note("sq", (l, j)))
                for h in range(2):
                    take(b, ("var", l, h), rs[:, halves(h)], h, func=ACT.Ln, bias=eps[:, :])
                for h in range(2):
                    act.wait_ge(S["ev"], at("ev", ("var", l, h), b))
                    nc.scalar.activation(rs[:, halves(h)], rs[:, halves(h)], ACT.Exp, scale=-0.5).then_inc(
                        S["rs"], note("rs", (l, h)))
                for j in range(J):
                    act.wait_ge(S["nrm"], at("nrm", (l, j), b))
                    nc.scalar.activation(y[:, j, :], y[:, j, :], ACT.Identity, scale=lnw[:, l, j:j + 1],
                                         bias=lnb[:, l, j:j + 1]).then_inc(S["aff"], note("aff", (l, j)))
                for c in range(2):
                    for h in range(2):
                        take(b, ("out", l, c, h), o2[:, c, halves(h)], h, rows=CH)

            act.wait_ge(loaded, 16 * LOADS)
            nc.scalar.activation(a0[:, :], a0[:, :], ACT.Exp).then_inc(exp_a, 1)
            nc.scalar.activation(a1[:, :], a1[:, :], ACT.Exp).then_inc(exp_a, 1)
            act.wait_ge(setup, 8)
            with act.Fori(0, NB) as b:
                front(b, 0)
                scans0(b)
                tail(b, 0)
                front(b, 1)
                scans1(b)
                tail(b, 1)

        @block.gpsimd
        def _(pool):
            def prepare_dt(b, l, i, j):
                delta = delta0[:, i % 2, j, :] if l == 0 else delta1[:, j, :]
                du = du0[:, i % 2, j, :] if l == 0 else du1[:, j, :]
                src = ordered[:, j, :] if l == 0 else u[:, j, :]
                pool.wait_ge(S["dl"], at("dl", (l, i, j), b))
                nc.gpsimd.tensor_tensor(du, delta, src, ALU.mult).then_inc(S["du"], note("du", (l, i, j)))

            def pair0(b, i, it, first, end):
                for p in range(2):
                    G = b * (K * N) + i * N + it * 2 + p
                    GS = b * NB_SPREAD + i * N + it * 2 + p
                    for j in range(J):
                        if first and p == 0:
                            pool.wait_ge(S["du"], at("du", (0, i, j), b))
                        if not (i == 0 and first):
                            pool.wait_ge(summed[j], G - 1)
                        if j == 0:
                            pool.wait_ge(B_ready, GS * 2 + 2)
                        nc.gpsimd.tensor_tensor(state0[:, p, j, :], du0[:, i % 2, j, :], B_all[:, p, :],
                                                ALU.mult).then_inc(source_ready[j], 1)

            def scans0(b):
                for j in range(J):
                    prepare_dt(b, 0, 0, j)
                for i in range(K):
                    for s, (lo, hi) in enumerate(PIECES):
                        if hi - lo == 1:
                            pair0(b, i, lo, lo == 0, hi == PAIRS)
                        else:
                            with pool.Fori(lo, hi) as it:
                                pair0(b, i, it, False, False)
                        if i < K - 1 and 1 <= s < 4:
                            prepare_dt(b, 0, i + 1, s - 1)

            def pair1(b, j, it, first, end):
                for p in range(2):
                    G = b * (J * N) + j * N + it * 2 + p
                    GS = b * NB_SPREAD + (K * N + j * N) + it * 2 + p
                    if first and p == 0:
                        pool.wait_ge(S["du"], at("du", (1, 0, j), b))
                    if not (j == 0 and first):
                        pool.wait_ge(dve1_ready, G - 1)
                        pool.wait_ge(pool1_ready, G * 3 - 3)
                    pool.wait_ge(B_ready, GS * 2 + 2)
                    nc.gpsimd.tensor_tensor(src1[:, p, :], du1[:, j, :], B_all[:, p, :],
                                            ALU.mult).then_inc(src1_ready, 1)
                    pool.wait_ge(src1_ready, G + 1)
                    for q in (0, 1, 3):
                        pool.wait_ge(gate1_ready, G * 4 + (q + 1))
                        state, src = state1[:, p, q, :], src1[:, p, :]
                        if q == 3:
                            state = state.rearrange("p (c r) -> p c r", c=SIDE)
                            src = src.rearrange("p (r c) -> p c r", r=SIDE)
                        nc.gpsimd.tensor_tensor(state, state, src, ALU.mult).then_inc(pool1_ready, 1)

            def scans1(b):
                for j in range(J):
                    prepare_dt(b, 1, 0, j)
                for j in range(J):
                    pair1(b, j, 0, True, False)
                    with pool.Fori(1, PAIRS - 1) as it:
                        pair1(b, j, it, False, False)
                    pair1(b, j, PAIRS - 1, False, True)

            with pool.Fori(0, NB) as b:
                scans0(b)
                scans1(b)

        @block.vector
        def _(dve):
            def front(b, l):
                if l == 0:
                    dve.wait_ge(load_x_done, b * 16 + 16)
                else:
                    dve.wait_ge(S["res"], at("res", (0, 1), b))
                for c in range(2):
                    for h in range(2):
                        nc.vector.bn_stats(stats[:, c, h, :], xT[:, c, halves(h)]).then_inc(
                            S["stat"], note("stat", (l, "bn")))
                dve.wait_ge(S["stat"], at("stat", (l, "bn"), b))
                nc.vector.memset(sq2[:, :], 0.0).then_inc(S["stat"], note("stat", (l, "carrier")))
                for c in range(2):
                    nc.vector.bn_aggr(mv[:, c, :], stats[:, c, :, :]).then_inc(S["stat"], note("stat", (l, "mv")))
                dve.wait_ge(S["stat"], at("stat", (l, "mv"), b))
                nc.vector.tensor_tensor(sq2[:, :], mv[:, :, 0], mv[:, :, 0], ALU.mult).then_inc(
                    S["stat"], note("stat", (l, "m2")))
                dve.wait_ge(S["stat"], at("stat", (l, "m2"), b))
                nc.vector.tensor_tensor(mv[:, :, 1], mv[:, :, 1], sq2[:, :], ALU.add).then_inc(
                    S["stat"], note("stat", (l, "msq")))
                dve.wait_ge(S["ev"], at("ev", ("gn", l), b))
                dve.wait_ge(S["stat"], at("stat", (l, "msq"), b))
                nc.vector.tensor_tensor(sq2[:, :], gs[:, :, 0], gs[:, :, 0], ALU.mult).then_inc(
                    S["stat"], note("stat", (l, "gm2")))
                dve.wait_ge(S["stat"], at("stat", (l, "gm2"), b))
                nc.vector.tensor_tensor(gvar[:, :], gs[:, :, 1], sq2[:, :], ALU.subtract).then_inc(
                    S["stat"], note("stat", (l, "gvar")))
                dve.wait_ge(S["gs"], at("gs", (l, "rstd"), b))
                for c in range(2):
                    nc.vector.tensor_scalar(xn[:, c, :], xT[:, c, :], gs[:, c, 0:1], rstd[:, c:c + 1],
                                            ALU.subtract, ALU.mult).then_inc(S["xn"], note("xn", (l, c)))
                for border in (padded[:, :, 0, :], padded[:, :, PAD - 1, :],
                               padded[:, :, 1:PAD - 1, 0], padded[:, :, 1:PAD - 1, PAD - 1]):
                    nc.vector.memset(border, 0.0).then_inc(S["pad"], note("pad", l))
                for tap in range(9):
                    dr, dc = tap // 3, tap % 3
                    for j in range(J):
                        dst = u[:, j, :].rearrange("p (r c) -> p r c", c=SIDE)
                        src = padded[:, j, dr:dr + SIDE, dc:dc + SIDE]
                        if tap == 0:
                            dve.wait_ge(S["pad"], at("pad", l, b))
                            dve.wait_ge(S["ev"], at("ev", ("in", l, j, 1), b))
                            ins = nc.vector.tensor_scalar(dst, src, cw[:, l, j, 0:1], cb[:, l, j:j + 1],
                                                          ALU.mult, ALU.add)
                        else:
                            dve.wait_ge(S["conv"], at("conv", (l, j, tap - 1), b))
                            ins = nc.vector.scalar_tensor_tensor(dst, src, cw[:, l, j, tap:tap + 1], dst,
                                                                 ALU.mult, ALU.add)
                        ins.then_inc(S["conv"], note("conv", (l, j, tap)))

            def prepare_bc(b, l, i):
                slot = parts[:, i % 2, :]
                dve.wait_ge(S["p1"], at("p1", (l, i), b))
                nc.vector.tensor_tensor(xdbl[0:XR, :], xdbl[0:XR, :], slot[:, :], ALU.subtract).then_inc(
                    S["r1"], note("r1", (l, i)))
                dve.wait_ge(S["p2"], at("p2", (l, i), b))
                dve.wait_ge(S["r1"], at("r1", (l, i), b))
                nc.vector.tensor_tensor(slot[64:96, :], xdbl[64:96, :], slot[64:96, :], ALU.subtract).then_inc(
                    S["parts"], note("parts", (l, i)))

            def prepare_dt(b, l, i, j):
                delta = delta0[:, i % 2, j, :] if l == 0 else delta1[:, j, :]
                e = du0[:, i % 2, j, :] if l == 0 else du1[:, j, :]
                log_w, w = soft[l][:, 0, :], soft[l][:, 1, :]
                dve.wait_ge(S["w1"], at("w1", (l, i, j), b))
                nc.vector.scalar_tensor_tensor(log_w, w, 1.0, log_w, ALU.subtract, ALU.subtract).then_inc(
                    S["q"], note("q", (l, i, j)))
                dve.wait_ge(S["q"], at("q", (l, i, j), b))
                nc.vector.tensor_tensor(e, e, log_w, ALU.subtract).then_inc(S["g"], note("g", (l, i, j)))
                dve.wait_ge(S["g"], at("g", (l, i, j), b))
                nc.vector.scalar_tensor_tensor(delta, delta, 0.0, e, ALU.max, ALU.add).then_inc(
                    S["dl"], note("dl", (l, i, j)))

            def pair0(b, i, it, first, end):
                back = SCANS[i][2]
                for p in range(2):
                    G = b * (K * N) + i * N + it * 2 + p
                    GS = b * NB_SPREAD + i * N + it * 2 + p

                    def run(ap):
                        return ap[:, ::-1] if back else ap

                    def scan(j):
                        dve.wait_ge(decay_ready[j], G + 1)
                        dve.wait_ge(source_ready[j], G + 1)
                        state = run(state0[:, p, j, :])
                        nc.vector.tensor_tensor_scan(state, run(decay0[:, j, :]), state, 0.0,
                                                     ALU.mult, ALU.add).then_inc(scanned[j], 1)

                    def weigh(j):
                        dve.wait_ge(scanned[j], G + 1)
                        if j == 0:
                            dve.wait_ge(C_ready, GS * 2 + 2)
                        state = state0[:, p, j, :]
                        nc.vector.tensor_tensor(state, state, C_all[:, p, :], ALU.mult).then_inc(weighted[j], 1)

                    scan(0)
                    scan(1)
                    weigh(0)
                    scan(2)
                    weigh(1)
                    weigh(2)

            def collect0(b, i):
                for j in range(J):
                    dve.wait_ge(summed[j], b * (K * N) + (i + 1) * N)
                    if i < 2:
                        dve.wait_ge(S["yinit"], at("yinit", (0, j), b))
                    else:
                        before = max(q for q in range(i) if closes(q))
                        dve.wait_ge(S["yev"], at("yev", (0, before, j), b))
                    acc = yacc0[:, j, :, :].rearrange("p h t -> p (h t)")
                    for dst, src in zip(lines(y[:, j, :], SCANS[i][1]), stored(acc)):
                        nc.vector.tensor_tensor(dst, dst, src, ALU.add).then_inc(S["yev"], note("yev", (0, i, j)))

            def scans0(b):
                prepare_bc(b, 0, 0)
                for j in range(J):
                    prepare_dt(b, 0, 0, j)
                for i in range(K):
                    for s, (lo, hi) in enumerate(PIECES):
                        if hi - lo == 1:
                            pair0(b, i, lo, lo == 0, hi == PAIRS)
                        else:
                            with dve.Fori(lo, hi) as it:
                                pair0(b, i, it, False, False)
                        if i < K - 1 and s < 4:
                            if s == 0:
                                prepare_bc(b, 0, i + 1)
                            else:
                                prepare_dt(b, 0, i + 1, s - 1)
                    if closes(i):
                        collect0(b, i)

            def weigh1(b, j, G, GS, slot, start):
                dve.wait_ge(hsum_ready, G * 4)
                dve.wait_ge(C_ready, GS * 2)
                if not start:
                    dve.wait_ge(summed1, G - 1)
                nc.vector.tensor_tensor(yc1[:, slot, :], hsum[:, slot, :, :].rearrange("p h t -> p (h t)"),
                                        C_all[:, slot, :], ALU.mult).then_inc(weighted1, 1)

            def pair1(b, j, it, first, end):
                for p in range(2):
                    G = b * (J * N) + j * N + it * 2 + p
                    GS = b * NB_SPREAD + (K * N + j * N) + it * 2 + p

                    def scan(q):
                        dve.wait_ge(decay1_ready, G * 2 + (1 + q // 2))
                        state, decay = state1[:, p, q, :], decay1[:, p, q // 2, :]
                        if q % 2:
                            state, decay = state[:, ::-1], decay[:, ::-1]
                        nc.vector.tensor_tensor_scan(state, decay, state, 0.0, ALU.mult, ALU.add).then_inc(scanned1, 1)

                    dve.wait_ge(pool1_ready, G * 3 + 1)
                    scan(0)
                    dve.wait_ge(pool1_ready, G * 3 + 2)
                    scan(1)
                    dve.wait_ge(gate1_ready, G * 4 + 3)
                    dve.wait_ge(src1_ready, G + 1)
                    state = state1[:, p, 2, :].rearrange("p (c r) -> p c r", c=SIDE)
                    nc.vector.tensor_tensor(state, state, src1[:, p, :].rearrange("p (r c) -> p c r", r=SIDE),
                                            ALU.mult).then_inc(dve1_ready, 1)
                    if not (first and p == 0):
                        weigh1(b, j, G, GS, 1 - p, j == 0 and first)
                    dve.wait_ge(dve1_ready, G + 1)
                    scan(2)
                    dve.wait_ge(pool1_ready, G * 3 + 3)
                    scan(3)

            def scans1(b):
                prepare_bc(b, 1, 0)
                for j in range(J):
                    prepare_dt(b, 1, 0, j)
                for j in range(J):
                    dve.wait_ge(S["dl"], at("dl", (1, 0, j), b))
                    nc.vector.tensor_copy(delta_cols.rearrange("p (c r) -> p c r", c=SIDE),
                                          delta1[:, j, :].rearrange("p (r c) -> p c r", r=SIDE)).then_inc(
                        S["dc"], note("dc", j))
                    dve.wait_ge(S["dc"], at("dc", j, b))
                    for q in range(Q):
                        src, dst = delta1[:, j, :] if q < 2 else delta_cols, csum[:, q, :]
                        if q % 2:
                            src, dst = src[:, ::-1], dst[:, ::-1]
                        nc.vector.tensor_tensor_scan(dst, one[:, :].broadcast_to([P, T]), src, 0.0,
                                                     ALU.mult, ALU.add).then_inc(S["cs"], note("cs", (j, q)))
                    dve.wait_ge(S["cs"], at("cs", (j, Q - 1), b))
                    pair1(b, j, 0, True, False)
                    with dve.Fori(1, PAIRS - 1) as it:
                        pair1(b, j, it, False, False)
                    pair1(b, j, PAIRS - 1, False, True)
                    G = b * (J * N) + (j + 1) * N
                    weigh1(b, j, G, b * NB_SPREAD + (K * N + (j + 1) * N), 1, False)
                    dve.wait_ge(summed1, G)
                    dve.wait_ge(S["yinit"], at("yinit", (1, j), b))
                    nc.vector.tensor_tensor(y[:, j, :], y[:, j, :], yacc1[:, :, :].rearrange("p h t -> p (h t)"),
                                            ALU.add).then_inc(S["yev"], note("yev", (1, j)))

            def tail(b, l):
                dve.wait_ge(S["ev"], at("ev", ("mu", l, 1), b))
                for j in range(J):
                    nc.vector.tensor_tensor(y[:, j, :], y[:, j, :], mu[:, :], ALU.subtract).then_inc(
                        S["cen"], note("cen", (l, j)))
                dve.wait_ge(S["rs"], at("rs", (l, 1), b))
                for j in range(J):
                    nc.vector.tensor_tensor(y[:, j, :], y[:, j, :], rs[:, :], ALU.mult).then_inc(
                        S["nrm"], note("nrm", (l, j)))
                for j in range(J):
                    dve.wait_ge(S["aff"], at("aff", (l, j), b))
                    nc.vector.tensor_tensor(y[:, j, :], y[:, j, :], gate[:, j, :], ALU.mult).then_inc(
                        S["gat"], note("gat", (l, j)))
                for c in range(2):
                    dve.wait_ge(S["ev"], at("ev", ("out", l, c, 1), b))
                    nc.vector.tensor_tensor(xT[:, c, :], xT[:, c, :], o2[:, c, :], ALU.add).then_inc(
                        S["res"], note("res", (l, c)))

            dve.wait_ge(loaded, 16 * LOADS)
            nc.vector.memset(one[:, :], 1.0).then_inc(setup, 1)
            nc.vector.memset(eps[:, :], 1e-5).then_inc(setup, 1)
            nc.vector.memset(guard[:, :], LN_1E12).then_inc(setup, 1)
            nc.vector.tensor_copy(pick_row[:, :], pick_f[:, :]).then_inc(setup, 1)
            nc.vector.tensor_reduce(skip[:, 0, :], dk[:, :, :], mybir.AxisListType.X, ALU.add).then_inc(setup, 1)
            nc.vector.tensor_scalar(skip[:, 1, :], skip[:, 1, :], float(Q), None, ALU.mult).then_inc(setup, 1)
            dve.wait_ge(exp_a, 2)
            nc.vector.tensor_scalar(a0[:, :], a0[:, :], -1.0, None, ALU.mult).then_inc(setup, 1)
            nc.vector.tensor_scalar(a1[:, :], a1[:, :], -1.0, None, ALU.mult).then_inc(setup, 1)
            dve.wait_ge(setup, 8)
            with dve.Fori(0, NB) as b:
                front(b, 0)
                scans0(b)
                tail(b, 0)
                front(b, 1)
                scans1(b)
                tail(b, 1)


def kernel(**inputs):
    import numpy as np
    import concourse.bacc as bacc
    from concourse.bass_utils import run_bass_kernel_spmd

    v = {k: np.asarray(a) for k, a in inputs.items()}
    L0, L1 = "L0_conv_", "L1_conv_"

    def channels(a):
        return np.moveaxis(a.reshape(J, P, *a.shape[1:]), 0, 1)

    def three(w):
        return channels(np.concatenate([w[:, R:]] * 3 + [w[:, :R]], axis=1))

    group = np.zeros((CH, CH), np.float32)
    size = C // 32
    for g in range(CH // size):
        group[g * size:(g + 1) * size, g * size:(g + 1) * size] = 1.0 / size
    arrays = {
        "x": v["x"].reshape(-1, T, C).transpose(0, 2, 1),
        "w_in": np.stack([v[L0 + "W_in"].T, v[L1 + "W_in"]]),
        "conv_w": np.stack([channels(v[l + "conv_w"].reshape(DI, 9)) for l in (L0, L1)], axis=1),
        "conv_b": np.stack([channels(v[l + "conv_b"]) for l in (L0, L1)], axis=1),
        "w_x0": np.stack([three(v[L0 + "x_proj_weight"][k].T) for k in range(K)]),
        "w_dt0": v[L0 + "dt_projs_weight"].transpose(0, 2, 1),
        "dt_b0": np.stack([channels(v[L0 + "dt_projs_bias"][k]) for k in range(K)], axis=1),
        "a_log0": v[L0 + "A_logs"].reshape(K, J, P, N).transpose(2, 0, 1, 3).reshape(P, K * J * N),
        "d0": v[L0 + "Ds"].reshape(K, J, P).transpose(2, 1, 0),
        "w_x1": three(v[L1 + "W_x"]),
        "w_dt1": v[L1 + "W_dt"],
        "dt_b1": channels(v[L1 + "b_dt"]),
        "a_log1": channels(v[L1 + "A_log"]).reshape(P, J * N),
        "d1": channels(v[L1 + "D_param"]),
        "ln_w": np.stack([channels(v[L0 + "ln_w"]), channels(v[L1 + "gamma"])], axis=1),
        "ln_b": np.stack([channels(v[L0 + "ln_b"]), channels(v[L1 + "beta"])], axis=1),
        "w_out": np.stack([v[L0 + "W_out"].T, v[L1 + "W_out"]]),
        "group_mean": group,
        "eye": np.eye(P, dtype=np.float32),
        "pick": np.tile(np.eye(2 * N, dtype=np.float32), (3, 1)),
        "mean_one": np.full((P, P), 1.0 / DI, np.float32),
    }
    arrays = {k: np.ascontiguousarray(a) for k, a in arrays.items()}

    def build(counts):
        nc = bacc.Bacc("TRN2", target_bir_lowering=False, num_devices=1)
        ins = {k: nc.dram_tensor("in_" + k, a.shape, mybir.dt.from_np(a.dtype), kind="ExternalInput").ap()
               for k, a in arrays.items()}
        out = nc.dram_tensor("out_x", arrays["x"].shape, F32, kind="ExternalOutput").ap()
        program(nc, counts, out=out, **ins)
        return nc

    first = Counts()
    build(first)
    nc = build(Counts(first))
    r = run_bass_kernel_spmd(nc, [{"in_" + k: a for k, a in arrays.items()}], core_ids=[0])
    y = np.asarray(r.results[0]["out_x"])
    return np.ascontiguousarray(y.transpose(0, 2, 1)).reshape(v["x"].shape)
```

```python
import concourse.bass as bass
from concourse import mybir
from contextlib import ExitStack

F32 = mybir.dt.float32
BF16 = mybir.dt.bfloat16
ALU = mybir.AluOpType
ACT = mybir.ActivationFunctionType

P = 128
NB, SIDE, C, DI, N, R, K = 8, 32, 192, 384, 16, 12, 8
T = SIDE * SIDE
HT = T // 2
CH = C // 2
J = DI // P
XR = 6 * N
PAD = SIDE + 2
PAIRS = N // 2
Q = 4

SCANS = [(0, "rows", False), (4, "rows", True), (3, "mirror", False), (7, "mirror", True),
         (1, "cols", False), (5, "cols", True), (2, "cols", True), (6, "cols", False)]
PIECES = [(0, 1), (1, 2), (2, 4), (4, 6), (6, 7), (7, 8)]
LN_1E12 = 27.631021115928547


def opens(i):
    return i == 0 or SCANS[i][1] != SCANS[i - 1][1]


def closes(i):
    return i == K - 1 or SCANS[i][1] != SCANS[i + 1][1]


def lines(ap, order):
    if order == "cols":
        v = ap.rearrange("p (r i two) -> p two i r", r=SIDE, two=2)
    else:
        v = ap.rearrange("p (i two c) -> p two i c", two=2, c=SIDE)
    if order == "mirror":
        return v[:, 0, :, ::-1], v[:, 1, :, :]
    return v[:, 0, :, :], v[:, 1, :, ::-1]


def stored(ap):
    v = ap.rearrange("p (i two c) -> p two i c", two=2, c=SIDE)
    return v[:, 0, :, :], v[:, 1, :, :]


class Counts:

    def __init__(self, known=None):
        self.known, self.now, self.marks = known, {}, {}

    def note(self, kind, step, by=1):
        self.now[kind] = self.now.get(kind, 0) + by
        self.marks[kind, step] = self.now[kind]
        return by

    def at(self, kind, step, b):
        if self.known is None:
            return 1
        return b * self.known.now[kind] + self.known.marks[kind, step]


def program(nc, counts, x, out, w_in, conv_w, conv_b, w_x0, w_dt0, dt_b0, a_log0, d0,
            w_x1, w_dt1, dt_b1, a_log1, d1, ln_w, ln_b, w_out, group_mean, eye, pick, mean_one):
    ctx = ExitStack()
    with ctx:
        def sb(name, shape, dt=F32):
            return ctx.enter_context(nc.sbuf_tensor(name, shape, dt))

        def semaphore(name):
            return ctx.enter_context(nc.semaphore(name))

        identity = sb("identity", [P, P])
        mean_ones = sb("mean_ones", [P, P])
        groups = sb("groups", [CH, CH])
        pick_f = sb("pick_f", [XR, 2 * N])
        pick_row = sb("pick_row", [XR, 2 * N], BF16)
        one = sb("one", [P, 1])
        cw = sb("cw", [P, 2, J, 9])
        cb = sb("cb", [P, 2, J])
        wx = sb("wx", [P, 2, J, XR + R])
        wdt = sb("wdt", [XR + R, 2, DI])
        wx1 = sb("wx1", [P, J, XR + R])
        wdt1 = sb("wdt1", [XR + R, DI])
        dtb0 = sb("dtb0", [P, K, J])
        dtb1 = sb("dtb1", [P, J])
        a0 = sb("a0", [P, K * J * N])
        a1 = sb("a1", [P, J * N])
        a1_now = sb("a1_now", [P, 2])
        dk = sb("dk", [P, J, K])
        skip = sb("skip", [P, 2, J])
        lnw = sb("lnw", [P, 2, J])
        lnb = sb("lnb", [P, 2, J])
        xT = sb("xT", [CH, 2, T])
        gate = sb("gate", [P, J, T])
        u = sb("u", [P, J, T])
        y = sb("y", [P, J, T])
        B_all = sb("B_all", [P, 2, T])
        C_all = sb("C_all", [P, 2, T])
        parts = sb("parts", [XR, 2, T], BF16)
        xdbl = sb("xdbl", [XR + R, T])
        stats = sb("stats", [CH, 2, 2, 6])
        mv = sb("mv", [CH, 2, 2])
        sq2 = sb("sq2", [CH, 2])
        gs = sb("gs", [CH, 2, 2])
        gvar = sb("gvar", [CH, 2])
        rstd = sb("rstd", [CH, 2])
        room = sb("room", [P, 31, T])
        ordered = room[:, 0:3, :]
        delta0 = room[:, 3:9, :].rearrange("p (s j) t -> p s j t", s=2)
        du0 = room[:, 9:15, :].rearrange("p (s j) t -> p s j t", s=2)
        decay0 = room[:, 19:25, :].rearrange("p (s j) t -> p s j t", s=2)
        state0 = room[:, 25:31, :].rearrange("p (s j) t -> p s j t", s=2)
        delta1 = room[:, 0:3, :]
        du1 = room[:, 3:6, :]
        csum = [room[:, 6:10, :], room[:, 26:30, :]]
        decay1 = room[:, 10:14, :].rearrange("p (s o) t -> p s o t", s=2)
        src1 = room[:, 14:16, :]
        state1 = room[:, 16:24, :].rearrange("p (s q) t -> p s q t", s=2)
        yc1 = room[:, 24:26, :]
        delta_cols = room[:, 30, :]
        soft = [room[:, 15:19, :], room[:, 26:30, :]]
        win = room[0:CH, 0:2, :].rearrange("p a t -> p (a t)")[:, 0:4 * DI].rearrange("p (h m) -> p h m", h=2)
        taps = room[:, 3:7, :].rearrange("p a t -> p (a t)")[:, 0:9 * P].rearrange("p (k m) -> p k m", m=P)
        wout = room[:, 9, 0:J * C].rearrange("p (j c) -> p j c", j=J)
        xn = room[0:CH, 17:19, :]
        padded = room[:, 20:24, :].rearrange("p a t -> p (a t)")[:, 0:J * PAD * PAD].rearrange(
            "p (j r c) -> p j r c", j=J, r=PAD)
        mu = room[:, 20, :]
        rs = room[:, 21, :]
        sq = room[:, 22:25, :]
        o2 = room[0:CH, 17:19, :]

        bank = ctx.enter_context(nc.psum_tensor("bank", [P, 8, HT], F32))
        WORK = (6, 7)
        yacc0 = bank[:, 0:6, :].rearrange("p (j h) t -> p j h t", j=J)
        yacc1 = bank[:, 0:2, :]
        hsum = bank[:, 2:6, :].rearrange("p (s h) t -> p s h t", s=2)

        names = ["load_wx0", "load_wx1", "load_win1", "load_wout0", "load_wout1", "mm", "ev", "stat", "gs", "xn", "pad", "conv", "u",
                 "uo", "p1", "r1", "p2", "parts", "ab", "ex", "ln", "d", "g1", "g", "dl", "du",
                 "yinit", "yev", "cs", "dc", "cen", "sq", "lnv", "rs", "nrm", "aff", "gat", "res"]
        S = {n: semaphore("s_" + n) for n in names}
        note, at = counts.note, counts.at
        setup = semaphore("setup")
        loaded = semaphore("loaded")
        exp_a = semaphore("exp_a")
        load_x_done = semaphore("load_x_done")
        store_done = semaphore("store_done")
        decay_ready = [semaphore(f"decay_ready_tile{j}") for j in range(J)]
        source_ready = [semaphore(f"source_ready_tile{j}") for j in range(J)]
        scanned = [semaphore(f"scanned_tile{j}") for j in range(J)]
        weighted = [semaphore(f"weighted_tile{j}") for j in range(J)]
        summed = [semaphore(f"summed_tile{j}") for j in range(J)]
        B_spread = semaphore("B_spread")
        C_spread = semaphore("C_spread")
        B_ready = semaphore("B_ready")
        C_ready = semaphore("C_ready")
        taps_ready = semaphore("taps_ready")
        win0_loaded = semaphore("win0_loaded")
        a1_ready = semaphore("a1_ready")
        decay1_ready = semaphore("decay1_ready")
        gate1_ready = semaphore("gate1_ready")
        src1_ready = semaphore("src1_ready")
        pool1_ready = semaphore("pool1_ready")
        dve1_ready = semaphore("dve1_ready")
        scanned1 = semaphore("scanned1")
        hsum_ready = semaphore("hsum_ready")
        weighted1 = semaphore("weighted1")
        summed1 = semaphore("summed1")
        NB_SPREAD = K * N + J * N

        def halves(h):
            return slice(h * HT, (h + 1) * HT)

        block = ctx.enter_context(nc.Block())
        LOADS = 16

        @block.sync
        def _(sp):
            def load(dst, src):
                sp.dma_start(dst, src).then_inc(loaded, 16)

            load(groups[:, :], group_mean)
            load(identity[:, :], eye)
            load(pick_f[:, :], pick)
            load(dtb0[:, :, :], dt_b0)
            load(dtb1[:, :], dt_b1)
            load(a0[:, :], a_log0)
            load(a1[:, :], a_log1)
            load(dk[:, :, :], d0)
            load(skip[:, 1, :], d1)
            load(cw[:, :, :, :], conv_w)
            load(cb[:, :, :], conv_b)
            load(lnw[:, :, :], ln_w)
            load(lnb[:, :, :], ln_b)
            load(wx1[:, :, :], w_x1)
            load(wdt1[XR:XR + R, :], w_dt1)
            load(mean_ones[:, :], mean_one)
            def load_x(b):
                src = x[slice(b, b + 1) if isinstance(b, int) else bass.ds(b, 1), :, :]
                sp.dma_start(xT[:, :, :], src.rearrange("o (h p) t -> p (o h) t", p=CH)).then_inc(load_x_done, 16)

            def load_win(l, sem, by=16):
                sp.dma_start(win, w_in[l].rearrange("(h p) m -> p h m", p=CH)).then_inc(sem, by)

            def load_wout(l):
                kind = f"load_wout{l}"
                sp.dma_start(wout, w_out[l].rearrange("(j p) c -> p j c", p=P)).then_inc(S[kind], note(kind, 0, 16))

            def image(b, more):
                for i, (k, _, _) in enumerate(SCANS):
                    if i >= 2:
                        sp.wait_ge(S["ev"], at("ev", ("dt", 0, i - 2, J - 1, 1), b))
                    slot = f"load_wx{i % 2}"
                    sp.dma_start(wx[:, i % 2, :, :], w_x0[k]).then_inc(S[slot], note(slot, i, 16))
                    sp.dma_start(wdt[XR:XR + R, i % 2, :], w_dt0[k]).then_inc(S[slot], note(slot, i, 16))
                sp.wait_ge(S["yev"], at("yev", (0, K - 1, J - 1), b))
                load_wout(0)
                load_win(1, S["load_win1"], note("load_win1", 0, 16))
                sp.wait_ge(S["yev"], at("yev", (1, J - 1), b))
                load_wout(1)
                if more:
                    load_win(0, win0_loaded)
                sp.wait_ge(S["res"], at("res", (1, 1), b))
                dst = out[slice(b, b + 1) if isinstance(b, int) else bass.ds(b, 1), :, :]
                sp.dma_start(dst.rearrange("o (h p) t -> p (o h) t", p=CH), xT[:, :, :]).then_inc(store_done, 16)
                sp.wait_ge(store_done, b * 16 + 16)

            load_x(0)
            load_win(0, win0_loaded)
            before = dict(counts.now)
            if NB > 1:
                with sp.Fori(0, NB - 1) as b:
                    image(b, True)
                    load_x(b + 1)
            counts.now = before
            image(NB - 1, False)

        @block.tensor
        def _(pe):
            last = {}

            def work(b, h, step, waits, products, rows=P, cols=HT):
                free = last[h](b) if last[h] else None
                ev_waits = [w for w in waits if w[0] == "ev"]
                if free and not (ev_waits and free[0] is S["ev"]):
                    pe.wait_ge(*free)
                for kind, s in waits:
                    pe.wait_ge(S[kind], at(kind, s, b))
                for i, (lhsT, rhs) in enumerate(products):
                    ins = nc.tensor.matmul(bank[0:rows, WORK[h], 0:cols], lhsT, rhs,
                                           start=(i == 0), stop=(i == len(products) - 1))
                ins.then_inc(S["mm"], note("mm", step))
                last[h] = lambda b, step=step: (S["ev"], at("ev", step, b))

            def front(b, l):
                work(b, 0, ("gn", l), [("stat", (l, "msq"))],
                     [(groups[:, :], mv[:, :, :].rearrange("p h s -> p (h s)"))], rows=CH, cols=4)
                if l == 0:
                    pe.wait_ge(win0_loaded, b * 16 + 16)
                else:
                    pe.wait_ge(S["load_win1"], at("load_win1", 0, b))
                for m in range(2 * J):
                    for h in range(2):
                        work(b, h, ("in", l, m, h), [("xn", (l, 1))],
                             [(win[:, c, m * P:(m + 1) * P], xn[:, c, halves(h)]) for c in range(2)])
                pe.wait_ge(taps_ready, b * 2 + (l + 1))
                pe.wait_ge(S["pad"], at("pad", l, b))
                for h in range(2):
                    r0 = h * (SIDE // 2)
                    work(b, h, ("conv", l, h), [],
                         [(taps[:, t, :],
                           padded[:, J - 1, r0 + t // 3:r0 + t // 3 + SIDE // 2, t % 3:t % 3 + SIDE])
                          for t in range(9)])

            def prepare_bc(b, l, i):
                src = ordered if l == 0 else u
                w = wx[:, i % 2, :, :] if l == 0 else wx1
                waits = [("uo", max(o for o in range(i + 1) if opens(o))), (f"load_wx{i % 2}", i)] if l == 0 else [
                    ("u", (1, J - 2))]
                for h in range(2):
                    work(b, h, ("xd", l, i, h), waits,
                         [(w[:, j, :], src[:, j, halves(h)]) for j in range(J)], rows=XR + R)

            def prepare_dt(b, l, i, j):
                w = wdt[XR:XR + R, i % 2, :] if l == 0 else wdt1[XR:XR + R, :]
                for h in range(2):
                    work(b, h, ("dt", l, i, j, h), [("ev", ("xd", l, i, h))] if l == 0 and i > 0 and j == 0 else [],
                         [(w[:, j * P:(j + 1) * P], xdbl[XR:XR + R, halves(h)])])

            def spread(row, par, sem):
                for h in range(2):
                    ins = nc.tensor.matmul(bank[:, WORK[h], :], pick_row[:, row].broadcast_to([XR, P]),
                                           parts[:, par, halves(h)], start=True, stop=True)
                ins.then_inc(sem, 1)

            def add_state(b, G, j, p, start, stop):
                for h in range(2):
                    ins = nc.tensor.matmul(yacc0[:, j, h, :], identity[:, :], state0[:, p, j, halves(h)],
                                           start=start, stop=stop)
                ins.then_inc(summed[j], 1)

            def step(b, i, n):
                if i == K - 1 or n not in (1, 2, 7, 11):
                    return None
                done = b * NB_SPREAD + (i * N + n + 2)
                for h in range(2):
                    last[h] = lambda b, v=done: (C_ready, v)
                if n == 1:
                    prepare_bc(b, 0, i + 1)
                    return "xd", 0, i + 1, 1
                j = (2, 7, 11).index(n)
                prepare_dt(b, 0, i + 1, j)
                return "dt", 0, i + 1, j, 1

            def pair0(b, i, it, prepared=None):
                for p in range(2):
                    n = it * 2 + p
                    static = isinstance(n, int)
                    G = b * (K * N) + i * N + it * 2 + p
                    GS = b * NB_SPREAD + i * N + it * 2 + p
                    ahead = [(2, 0, C_ready, GS + 1, B_spread),
                             (1, N, B_ready, GS + 3, C_spread)]
                    for lead, row0, sem, value, signal in ahead:
                        par, row = i % 2, n + lead
                        if static and row >= N:
                            if i == K - 1:
                                continue
                            par, row = (i + 1) % 2, row - N
                            if n == N - 2:
                                pe.wait_ge(S["parts"], at("parts", (0, i + 1), b))
                        if lead == 2 and prepared:
                            pe.wait_ge(S["ev"], at("ev", prepared, b))
                        if static and i == K - 1 and n == N - 2 and lead == 1:
                            pe.wait_ge(C_ready, GS + 1)
                        else:
                            pe.wait_ge(sem, value)
                        row = row + row0
                        spread(slice(row, row + 1) if static else bass.ds(row, 1), par, signal)
                    if p == 1 or static:
                        prepared = None
                    if static:
                        prepared = step(b, i, n)
                    start, stop = static and n == 0 and opens(i), static and n == N - 1 and closes(i)
                    for j in range(J):
                        if start and i > 0:
                            pe.wait_ge(S["yev"], at("yev", (0, i - 1, j), b))
                        pe.wait_ge(weighted[j], G + 1)
                        add_state(b, G, j, p, start, stop)
                return prepared

            def scans0(b):
                prepare_bc(b, 0, 0)
                for j in range(J):
                    prepare_dt(b, 0, 0, j)
                pe.wait_ge(S["parts"], at("parts", (0, 0), b))
                GS = b * NB_SPREAD
                pe.wait_ge(*last[1](b))
                spread(slice(0, 1), 0, B_spread)
                pe.wait_ge(B_ready, GS + 1)
                spread(slice(1, 2), 0, B_spread)
                pe.wait_ge(B_ready, GS + 2)
                spread(slice(N, N + 1), 0, C_spread)
                for i in range(K):
                    prepared = None
                    for lo, hi in PIECES:
                        if hi - lo == 1:
                            prepared = pair0(b, i, lo, prepared)
                        else:
                            with pe.Fori(lo, hi) as it:
                                pair0(b, i, it, prepared)
                            prepared = step(b, i, 2 * hi - 1)

            def pair1(b, j, it, first, end):
                for p in range(2):
                    n = it * 2 + p
                    G = b * (J * N) + j * N + it * 2 + p
                    GS = b * NB_SPREAD + (K * N + j * N) + it * 2 + p
                    is0 = first and p == 0
                    is15 = end and p == 1
                    if not is15:
                        sel = slice(n + 1, n + 2) if isinstance(n, int) else bass.ds(n + 1, 1)
                        if is0:
                            pe.wait_ge(B_ready, GS + 1)
                        else:
                            pe.wait_ge(C_ready, GS)
                        spread(sel, 0, B_spread)
                    selC = slice(n + N, n + N + 1) if isinstance(n, int) else bass.ds(n + N, 1)
                    if not is15:
                        pe.wait_ge(B_ready, GS + 2)
                    else:
                        pe.wait_ge(C_ready, GS)
                    spread(selC, 0, C_spread)
                    if not (first and j == 0):
                        pe.wait_ge(weighted1, G - 1)

                    def add_direction(q):
                        pe.wait_ge(scanned1, G * 4 + (q + 1))
                        for h in range(2):
                            if q < 2:
                                rhs = state1[:, p, q, halves(h)]
                            else:
                                rhs = state1[:, p, q, :].rearrange("p (c r) -> p r c", c=SIDE)[
                                    :, h * (SIDE // 2):(h + 1) * (SIDE // 2), :]
                            ins = nc.tensor.matmul(hsum[:, p, h, :], identity[:, :], rhs,
                                                   start=(q == 0), stop=(q == Q - 1))
                        ins.then_inc(hsum_ready, 1)

                    add_direction(0)
                    add_direction(1)
                    if not is0:
                        add_weighted(b, j, G, 1 - p, first and p == 1, False)
                    add_direction(2)
                    add_direction(3)

            def add_weighted(b, j, G, slot, start, stop):
                if start and j > 0:
                    pe.wait_ge(S["yev"], at("yev", (1, j - 1), b))
                pe.wait_ge(weighted1, G)
                for h in range(2):
                    ins = nc.tensor.matmul(yacc1[:, h, :], identity[:, :], yc1[:, slot, halves(h)],
                                           start=start, stop=stop)
                ins.then_inc(summed1, 1)

            def scans1(b):
                prepare_bc(b, 1, 0)
                for j in range(J):
                    prepare_dt(b, 1, 0, j)
                pe.wait_ge(S["parts"], at("parts", (1, 0), b))
                for j in range(J):
                    if j == 0:
                        pe.wait_ge(*last[1](b))
                    else:
                        pe.wait_ge(C_ready, b * NB_SPREAD + (K * N + j * N))
                    spread(slice(0, 1), 0, B_spread)
                    pair1(b, j, 0, True, False)
                    with pe.Fori(1, PAIRS - 1) as it:
                        pair1(b, j, it, False, False)
                    pair1(b, j, PAIRS - 1, False, True)
                    add_weighted(b, j, b * (J * N) + (j + 1) * N, 1, False, True)
                for h in range(2):
                    last[h] = lambda b: (C_ready, b * NB_SPREAD + NB_SPREAD)

            def tail(b, l):
                yev = [("yev", (0, K - 1, J - 1) if l == 0 else (1, J - 1))]
                for h in range(2):
                    work(b, h, ("mu", l, h), yev, [(mean_ones[:, :], y[:, j, halves(h)]) for j in range(J)])
                for h in range(2):
                    work(b, h, ("var", l, h), [("sq", (l, J - 1))],
                         [(mean_ones[:, :], sq[:, j, halves(h)]) for j in range(J)])
                pe.wait_ge(S[f"load_wout{l}"], at(f"load_wout{l}", 0, b))
                for c in range(2):
                    for h in range(2):
                        work(b, h, ("out", l, c, h), [("gat", (l, J - 1))],
                             [(wout[:, j, c * CH:(c + 1) * CH], y[:, j, halves(h)]) for j in range(J)],
                             rows=CH)

            pe.wait_ge(loaded, 16 * LOADS)
            pe.wait_ge(setup, 6)
            with pe.Fori(0, NB) as b:
                for h in range(2):
                    last[h] = None
                front(b, 0)
                scans0(b)
                for h in range(2):
                    last[h] = lambda b: (C_ready, b * NB_SPREAD + K * N)
                tail(b, 0)
                front(b, 1)
                scans1(b)
                tail(b, 1)

        @block.scalar
        def _(act):
            def take(b, step, dst, h, func=ACT.Copy, rows=P, cols=HT, src=None, **kw):
                act.wait_ge(S["mm"], at("mm", step, b))
                nc.scalar.activation(dst, bank[0:rows, WORK[h], 0:cols] if src is None else src, func,
                                     **kw).then_inc(S["ev"], note("ev", step))

            def front(b, l):
                take(b, ("gn", l), gs[:, :, :].rearrange("p h s -> p (h s)"), 0, rows=CH, cols=4)
                act.wait_ge(S["stat"], at("stat", (l, "gvar"), b))
                nc.scalar.activation(rstd[:, :], gvar[:, :], ACT.Ln, bias=1e-5).then_inc(
                    S["gs"], note("gs", (l, "ln")))
                act.wait_ge(S["gs"], at("gs", (l, "ln"), b))
                nc.scalar.activation(rstd[:, :], rstd[:, :], ACT.Exp, scale=-0.5).then_inc(
                    S["gs"], note("gs", (l, "rstd")))
                act.wait_ge(S["xn"], at("xn", (l, 1), b))
                for m in range(2 * J):
                    for h in range(2):
                        if m < J:
                            rows = slice(1 + h * (SIDE // 2), 1 + (h + 1) * (SIDE // 2))
                            take(b, ("in", l, m, h), padded[:, m, rows, 1:1 + SIDE], h,
                                 src=bank[:, WORK[h], :].rearrange("p (r c) -> p r c", c=SIDE))
                        else:
                            take(b, ("in", l, m, h), gate[:, m - J, halves(h)], h, func=ACT.Silu)
                for h in range(2):
                    take(b, ("conv", l, h), u[:, J - 1, halves(h)], h, func=ACT.Silu, bias=cb[:, l, J - 1:J])
                for j in range(J - 1):
                    act.wait_ge(S["conv"], at("conv", (l, j, 8), b))
                    nc.scalar.activation(u[:, j, :], u[:, j, :], ACT.Silu).then_inc(S["u"], note("u", (l, j)))
                for j in range(J):
                    if j < J - 1:
                        act.wait_ge(S["u"], at("u", (l, j), b))
                    else:
                        act.wait_ge(S["ev"], at("ev", ("conv", l, 1), b))
                    nc.scalar.activation(y[:, j, :], u[:, j, :], ACT.Copy, scale=skip[:, l, j:j + 1]).then_inc(
                        S["yinit"], note("yinit", (l, j)))

            def reorder(b, i):
                if i > 0:
                    act.wait_ge(S["du"], at("du", (0, i - 1, J - 1), b))
                for j in range(J):
                    for src, dst in zip(lines(u[:, j, :], SCANS[i][1]), stored(ordered[:, j, :])):
                        nc.scalar.activation(dst, src, ACT.Copy).then_inc(S["uo"], note("uo", i))

            def prepare_bc(b, l, i):
                for h in range(2):
                    take(b, ("xd", l, i, h), xdbl[:, halves(h)], h, rows=XR + R)
                slot = parts[:, i % 2, :]
                act.wait_ge(S["ev"], at("ev", ("xd", l, i, 1), b))
                nc.scalar.activation(slot[:, :], xdbl[0:XR, :], ACT.Copy).then_inc(S["p1"], note("p1", (l, i)))

            def second_part(b, l, i):
                slot = parts[:, i % 2, :]
                act.wait_ge(S["r1"], at("r1", (l, i), b))
                nc.scalar.activation(slot[32:64, :], xdbl[32:64, :], ACT.Copy).then_inc(S["p2"], note("p2", (l, i, 0)))
                nc.scalar.activation(slot[64:96, :], xdbl[64:96, :], ACT.Copy).then_inc(S["p2"], note("p2", (l, i)))

            def take_dt(b, l, i, j):
                delta = delta0[:, i % 2, j, :] if l == 0 else delta1[:, j, :]
                bias = dtb0[:, SCANS[i][0], j:j + 1] if l == 0 else dtb1[:, j:j + 1]
                for h in range(2):
                    take(b, ("dt", l, i, j, h), delta[:, halves(h)], h, func=ACT.Identity, bias=bias)

            def absolute(b, l, i, j):
                delta = delta0[:, i % 2, j, :] if l == 0 else delta1[:, j, :]
                e = du0[:, i % 2, j, :] if l == 0 else du1[:, j, :]
                act.wait_ge(S["ev"], at("ev", ("dt", l, i, j, 1), b))
                nc.scalar.activation(e, delta, ACT.Abs).then_inc(S["ab"], note("ab", (l, i, j)))

            def exponent(b, l, i, j):
                e = du0[:, i % 2, j, :] if l == 0 else du1[:, j, :]
                act.wait_ge(S["ab"], at("ab", (l, i, j), b))
                nc.scalar.activation(e, e, ACT.Exp, scale=-1.0).then_inc(S["ex"], note("ex", (l, i, j)))

            def logarithms(b, l, i):
                for j in range(J):
                    e = du0[:, i % 2, j, :] if l == 0 else du1[:, j, :]
                    act.wait_ge(S["ex"], at("ex", (l, i, j), b))
                    if j == 0 and i > 0:
                        act.wait_ge(S["dl"], at("dl", (l, i - 1, J - 1), b))
                    nc.scalar.activation(soft[l][:, j, :], e, ACT.Ln, bias=1.0).then_inc(
                        S["ln"], note("ln", (l, i, j)))

            def prepare_first(b, l):
                prepare_bc(b, l, 0)
                second_part(b, l, 0)
                for j in range(J):
                    take_dt(b, l, 0, j)
                for j in range(J):
                    absolute(b, l, 0, j)
                for j in range(J):
                    exponent(b, l, 0, j)
                logarithms(b, l, 0)

            def take_spread(GS, slot, sem_in, sem_out, dst):
                act.wait_ge(sem_in, GS + 1)
                nc.scalar.activation(dst[:, slot, :], bank[:, WORK[0]:WORK[1] + 1, :].rearrange("p h t -> p (h t)"),
                                     ACT.Copy).then_inc(sem_out, 1)

            def step(b, i, n):
                if i == K - 1:
                    return
                i = i + 1
                if n == 0 and opens(i):
                    reorder(b, i)
                if n == 1:
                    prepare_bc(b, 0, i)
                if n == 2:
                    take_dt(b, 0, i, 0)
                    absolute(b, 0, i, 0)
                if n == 3:
                    exponent(b, 0, i, 0)
                    second_part(b, 0, i)
                if n == 7:
                    take_dt(b, 0, i, 1)
                    absolute(b, 0, i, 1)
                if n == 11:
                    exponent(b, 0, i, 1)
                    take_dt(b, 0, i, 2)
                if n == 12:
                    absolute(b, 0, i, 2)
                    exponent(b, 0, i, 2)
                if n == 13:
                    logarithms(b, 0, i)

            def decays(b, i, n, it, p, fresh, G):
                for j in range(J):
                    if isinstance(n, int) and n == 0:
                        act.wait_ge(S["dl"], at("dl", (0, i, j), b))
                    if not fresh:
                        act.wait_ge(scanned[j], G - 1)
                    col = (SCANS[i][0] * J + j) * N + n
                    sel = slice(col, col + 1) if isinstance(col, int) else bass.ds(col, 1)
                    nc.scalar.activation(decay0[:, p, j, :], delta0[:, i % 2, j, :], ACT.Exp,
                                         scale=a0[:, sel]).then_inc(decay_ready[j], 1)

            def pair0(b, i, it):
                for p in range(2):
                    n = it * 2 + p
                    static = isinstance(n, int)
                    G = b * (K * N) + i * N + it * 2 + p
                    GS = b * NB_SPREAD + i * N + it * 2 + p
                    final = static and i == K - 1
                    if not (final and n == N - 1):
                        if static and n == N - 1:
                            decays(b, i + 1, 0, 0, 0, False, G + 1)
                        else:
                            decays(b, i, n + 1, it, 1 - p, static and i == 0 and n == 0, G + 1)
                    if not (final and n >= N - 2):
                        act.wait_ge(source_ready[J - 1], G + 1)
                        take_spread(GS + 2, p, B_spread, B_ready, B_all)
                    if not (final and n == N - 1):
                        if not (static and i == 0 and n == 0):
                            act.wait_ge(weighted[J - 1], G)
                        take_spread(GS + 1, 1 - p, C_spread, C_ready, C_all)
                    if static:
                        step(b, i, n)

            def scans0(b):
                reorder(b, 0)
                prepare_first(b, 0)
                GS = b * NB_SPREAD
                decays(b, 0, 0, 0, 0, True, 0)
                take_spread(GS, 0, B_spread, B_ready, B_all)
                take_spread(GS + 1, 1, B_spread, B_ready, B_all)
                take_spread(GS, 0, C_spread, C_ready, C_all)
                for i in range(K):
                    for lo, hi in PIECES:
                        if hi - lo == 1:
                            pair0(b, i, lo)
                        else:
                            with act.Fori(lo, hi) as it:
                                pair0(b, i, it)
                            step(b, i, 2 * hi - 1)

            def pair1(b, j, it, first, end):
                for p in range(2):
                    n = it * 2 + p
                    G = b * (J * N) + j * N + it * 2 + p
                    GS = b * NB_SPREAD + (K * N + j * N) + it * 2 + p
                    fresh = j == 0 and first
                    col = j * N + n
                    sel = slice(col, col + 1) if isinstance(col, int) else bass.ds(col, 1)
                    if not fresh:
                        act.wait_ge(gate1_ready, G * 4 - 4)
                    nc.scalar.activation(a1_now[:, p:p + 1], a1[:, sel], ACT.Copy).then_inc(a1_ready, 1)
                    if first and p == 0:
                        act.wait_ge(S["dl"], at("dl", (1, 0, j), b))
                    act.wait_ge(a1_ready, G + 1)
                    for o in range(2):
                        if not fresh:
                            act.wait_ge(scanned1, G * 4 - (8 - 2 * (o + 1)))
                        src = delta1[:, j, :]
                        dst = decay1[:, p, o, :]
                        if o == 1:
                            src = src.rearrange("p (r c) -> p c r", r=SIDE)
                            dst = dst.rearrange("p (c r) -> p c r", c=SIDE)
                        nc.scalar.activation(dst, src, ACT.Exp, scale=a1_now[:, p:p + 1]).then_inc(decay1_ready, 1)
                    for q in range(Q):
                        if first and p == 0:
                            act.wait_ge(S["cs"], at("cs", (j, q), b))
                        if not fresh:
                            act.wait_ge(hsum_ready, G * 4 - (8 - (q + 1)))
                        nc.scalar.activation(state1[:, p, q, :], csum[j % 2][:, q, :], ACT.Sigmoid,
                                             scale=a1_now[:, p:p + 1], bias=LN_1E12).then_inc(gate1_ready, 1)
                    if not (end and p == 1):
                        if not (j == 0 and first and p == 0):
                            act.wait_ge(src1_ready, G)
                        take_spread(GS + 1, 1 - p, B_spread, B_ready, B_all)
                    if not (first and j == 0):
                        act.wait_ge(weighted1, G - 1)
                    take_spread(GS, p, C_spread, C_ready, C_all)

            def scans1(b):
                prepare_first(b, 1)
                for j in range(J):
                    GS = b * NB_SPREAD + (K * N + j * N)
                    if j > 0:
                        act.wait_ge(src1_ready, b * (J * N) + j * N - 1)
                    take_spread(GS, 0, B_spread, B_ready, B_all)
                    pair1(b, j, 0, True, False)
                    with act.Fori(1, PAIRS - 1) as it:
                        pair1(b, j, it, False, False)
                    pair1(b, j, PAIRS - 1, False, True)

            def tail(b, l):
                for h in range(2):
                    take(b, ("mu", l, h), mu[:, halves(h)], h)
                for j in range(J):
                    act.wait_ge(S["cen"], at("cen", (l, j), b))
                    nc.scalar.activation(sq[:, j, :], y[:, j, :], ACT.Square).then_inc(S["sq"], note("sq", (l, j)))
                for h in range(2):
                    take(b, ("var", l, h), rs[:, halves(h)], h, func=ACT.Ln, bias=1e-5)
                for h in range(2):
                    act.wait_ge(S["ev"], at("ev", ("var", l, h), b))
                    nc.scalar.activation(rs[:, halves(h)], rs[:, halves(h)], ACT.Exp, scale=-0.5).then_inc(
                        S["rs"], note("rs", (l, h)))
                for j in range(J):
                    act.wait_ge(S["nrm"], at("nrm", (l, j), b))
                    nc.scalar.activation(y[:, j, :], y[:, j, :], ACT.Identity, scale=lnw[:, l, j:j + 1],
                                         bias=lnb[:, l, j:j + 1]).then_inc(S["aff"], note("aff", (l, j)))
                for c in range(2):
                    for h in range(2):
                        take(b, ("out", l, c, h), o2[:, c, halves(h)], h, rows=CH)

            act.wait_ge(loaded, 16 * LOADS)
            nc.scalar.activation(a0[:, :], a0[:, :], ACT.Exp).then_inc(exp_a, 1)
            nc.scalar.activation(a1[:, :], a1[:, :], ACT.Exp).then_inc(exp_a, 1)
            act.wait_ge(setup, 6)
            with act.Fori(0, NB) as b:
                front(b, 0)
                scans0(b)
                tail(b, 0)
                front(b, 1)
                scans1(b)
                tail(b, 1)

        @block.gpsimd
        def _(pool):
            def prepare_dt(b, l, i, j):
                delta = delta0[:, i % 2, j, :] if l == 0 else delta1[:, j, :]
                du = du0[:, i % 2, j, :] if l == 0 else du1[:, j, :]
                src = ordered[:, j, :] if l == 0 else u[:, j, :]
                pool.wait_ge(S["dl"], at("dl", (l, i, j), b))
                nc.gpsimd.tensor_tensor(du, delta, src, ALU.mult).then_inc(S["du"], note("du", (l, i, j)))

            def pair0(b, i, it, first, end):
                for p in range(2):
                    G = b * (K * N) + i * N + it * 2 + p
                    GS = b * NB_SPREAD + i * N + it * 2 + p
                    for j in range(J):
                        if first and p == 0:
                            pool.wait_ge(S["du"], at("du", (0, i, j), b))
                        if not (i == 0 and first):
                            pool.wait_ge(summed[j], G - 1)
                        if j == 0:
                            pool.wait_ge(B_ready, GS + 1)
                        nc.gpsimd.tensor_tensor(state0[:, p, j, :], du0[:, i % 2, j, :], B_all[:, p, :],
                                                ALU.mult).then_inc(source_ready[j], 1)

            def scans0(b):
                for j in range(J):
                    prepare_dt(b, 0, 0, j)
                for i in range(K):
                    for lo, hi in PIECES:
                        if hi - lo == 1:
                            pair0(b, i, lo, lo == 0, hi == PAIRS)
                        else:
                            with pool.Fori(lo, hi) as it:
                                pair0(b, i, it, False, False)
                    if i < K - 1:
                        for j in range(J):
                            prepare_dt(b, 0, i + 1, j)

            def pair1(b, j, it, first, end):
                for p in range(2):
                    G = b * (J * N) + j * N + it * 2 + p
                    GS = b * NB_SPREAD + (K * N + j * N) + it * 2 + p
                    if first and p == 0:
                        pool.wait_ge(S["du"], at("du", (1, 0, j), b))
                    if not (j == 0 and first):
                        pool.wait_ge(dve1_ready, G - 1)
                        pool.wait_ge(pool1_ready, G * 3 - 3)
                    pool.wait_ge(B_ready, GS + 1)
                    nc.gpsimd.tensor_tensor(src1[:, p, :], du1[:, j, :], B_all[:, p, :],
                                            ALU.mult).then_inc(src1_ready, 1)
                    pool.wait_ge(src1_ready, G + 1)
                    for q in (0, 1, 3):
                        pool.wait_ge(gate1_ready, G * 4 + (q + 1))
                        state, src = state1[:, p, q, :], src1[:, p, :]
                        if q == 3:
                            state = state.rearrange("p (c r) -> p c r", c=SIDE)
                            src = src.rearrange("p (r c) -> p c r", r=SIDE)
                        nc.gpsimd.tensor_tensor(state, state, src, ALU.mult).then_inc(pool1_ready, 1)

            def scans1(b):
                for j in range(J):
                    prepare_dt(b, 1, 0, j)
                for j in range(J):
                    pair1(b, j, 0, True, False)
                    with pool.Fori(1, PAIRS - 1) as it:
                        pair1(b, j, it, False, False)
                    pair1(b, j, PAIRS - 1, False, True)

            def make_taps(l):
                nc.gpsimd.tensor_tensor(
                    taps[:, :, :], identity[:, :].unsqueeze(1).broadcast_to([P, 9, P]),
                    cw[:, l, J - 1, :].unsqueeze(2).broadcast_to([P, 9, P]), ALU.mult).then_inc(taps_ready, 1)

            pool.wait_ge(loaded, 16 * LOADS)
            make_taps(0)
            with pool.Fori(0, NB) as b:
                scans0(b)
                pool.wait_ge(S["yev"], at("yev", (0, K - 1, J - 1), b))
                make_taps(1)
                scans1(b)
                pool.wait_ge(S["yev"], at("yev", (1, J - 1), b))
                make_taps(0)

        @block.vector
        def _(dve):
            def front(b, l):
                if l == 0:
                    dve.wait_ge(load_x_done, b * 16 + 16)
                else:
                    dve.wait_ge(S["res"], at("res", (0, 1), b))
                for c in range(2):
                    for h in range(2):
                        nc.vector.bn_stats(stats[:, c, h, :], xT[:, c, halves(h)]).then_inc(
                            S["stat"], note("stat", (l, "bn")))
                dve.wait_ge(S["stat"], at("stat", (l, "bn"), b))
                nc.vector.memset(sq2[:, :], 0.0).then_inc(S["stat"], note("stat", (l, "carrier")))
                for c in range(2):
                    nc.vector.bn_aggr(mv[:, c, :], stats[:, c, :, :]).then_inc(S["stat"], note("stat", (l, "mv")))
                dve.wait_ge(S["stat"], at("stat", (l, "mv"), b))
                nc.vector.tensor_tensor(sq2[:, :], mv[:, :, 0], mv[:, :, 0], ALU.mult).then_inc(
                    S["stat"], note("stat", (l, "m2")))
                dve.wait_ge(S["stat"], at("stat", (l, "m2"), b))
                nc.vector.tensor_tensor(mv[:, :, 1], mv[:, :, 1], sq2[:, :], ALU.add).then_inc(
                    S["stat"], note("stat", (l, "msq")))
                dve.wait_ge(S["ev"], at("ev", ("gn", l), b))
                dve.wait_ge(S["stat"], at("stat", (l, "msq"), b))
                nc.vector.tensor_tensor(sq2[:, :], gs[:, :, 0], gs[:, :, 0], ALU.mult).then_inc(
                    S["stat"], note("stat", (l, "gm2")))
                dve.wait_ge(S["stat"], at("stat", (l, "gm2"), b))
                nc.vector.tensor_tensor(gvar[:, :], gs[:, :, 1], sq2[:, :], ALU.subtract).then_inc(
                    S["stat"], note("stat", (l, "gvar")))
                dve.wait_ge(S["gs"], at("gs", (l, "rstd"), b))
                for c in range(2):
                    nc.vector.tensor_scalar(xn[:, c, :], xT[:, c, :], gs[:, c, 0:1], rstd[:, c:c + 1],
                                            ALU.subtract, ALU.mult).then_inc(S["xn"], note("xn", (l, c)))
                for border in (padded[:, :, 0, :], padded[:, :, PAD - 1, :],
                               padded[:, :, 1:PAD - 1, 0], padded[:, :, 1:PAD - 1, PAD - 1]):
                    nc.vector.memset(border, 0.0).then_inc(S["pad"], note("pad", l))
                for tap in range(9):
                    dr, dc = tap // 3, tap % 3
                    for j in range(J - 1):
                        dst = u[:, j, :].rearrange("p (r c) -> p r c", c=SIDE)
                        src = padded[:, j, dr:dr + SIDE, dc:dc + SIDE]
                        if tap == 0:
                            dve.wait_ge(S["pad"], at("pad", l, b))
                            dve.wait_ge(S["ev"], at("ev", ("in", l, j, 1), b))
                            ins = nc.vector.tensor_scalar(dst, src, cw[:, l, j, 0:1], cb[:, l, j:j + 1],
                                                          ALU.mult, ALU.add)
                        else:
                            dve.wait_ge(S["conv"], at("conv", (l, j, tap - 1), b))
                            ins = nc.vector.scalar_tensor_tensor(dst, src, cw[:, l, j, tap:tap + 1], dst,
                                                                 ALU.mult, ALU.add)
                        ins.then_inc(S["conv"], note("conv", (l, j, tap)))

            def first_rest(b, l, i):
                slot = parts[:, i % 2, :]
                dve.wait_ge(S["p1"], at("p1", (l, i), b))
                nc.vector.tensor_tensor(xdbl[0:XR, :], xdbl[0:XR, :], slot[:, :], ALU.subtract).then_inc(
                    S["r1"], note("r1", (l, i)))

            def third_part(b, l, i):
                slot = parts[:, i % 2, :]
                dve.wait_ge(S["p2"], at("p2", (l, i), b))
                dve.wait_ge(S["r1"], at("r1", (l, i), b))
                nc.vector.tensor_tensor(slot[64:96, :], xdbl[64:96, :], slot[64:96, :], ALU.subtract).then_inc(
                    S["parts"], note("parts", (l, i)))

            def prepare_dt(b, l, i, j):
                delta = delta0[:, i % 2, j, :] if l == 0 else delta1[:, j, :]
                e = du0[:, i % 2, j, :] if l == 0 else du1[:, j, :]
                log_w, d = soft[l][:, j, :], soft[l][:, J, :]
                if j > 0 or i > 0:
                    dve.wait_ge(S["g1"], at("g1", (l, i, j - 1) if j > 0 else (l, i - 1, J - 1), b))
                dve.wait_ge(S["ln"], at("ln", (l, i, j), b))
                nc.vector.tensor_scalar(d, e, 1.0, 1.0, ALU.add, ALU.subtract).then_inc(S["d"], note("d", (l, i, j)))
                dve.wait_ge(S["d"], at("d", (l, i, j), b))
                nc.vector.tensor_tensor(e, e, d, ALU.subtract).then_inc(S["g1"], note("g1", (l, i, j)))
                dve.wait_ge(S["g1"], at("g1", (l, i, j), b))
                nc.vector.tensor_tensor(e, e, log_w, ALU.add).then_inc(S["g"], note("g", (l, i, j)))
                dve.wait_ge(S["g"], at("g", (l, i, j), b))
                nc.vector.scalar_tensor_tensor(delta, delta, 0.0, e, ALU.max, ALU.add).then_inc(
                    S["dl"], note("dl", (l, i, j)))

            def step(b, i, n):
                if i == K - 1:
                    return
                if n == 2:
                    first_rest(b, 0, i + 1)
                if n == 7:
                    third_part(b, 0, i + 1)
                if n == 14:
                    prepare_dt(b, 0, i + 1, 0)
                if n == 15:
                    prepare_dt(b, 0, i + 1, 1)
                    prepare_dt(b, 0, i + 1, 2)

            def pair0(b, i, it, first):
                back = SCANS[i][2]
                for p in range(2):
                    G = b * (K * N) + i * N + it * 2 + p
                    GS = b * NB_SPREAD + i * N + it * 2 + p

                    def run(ap):
                        return ap[:, ::-1] if back else ap

                    def scan(j):
                        dve.wait_ge(decay_ready[j], G + 1)
                        dve.wait_ge(source_ready[j], G + 1)
                        state = run(state0[:, p, j, :])
                        nc.vector.tensor_tensor_scan(state, run(decay0[:, p, j, :]), state, 0.0,
                                                     ALU.mult, ALU.add).then_inc(scanned[j], 1)

                    def weigh(j):
                        dve.wait_ge(scanned[j], G + 1)
                        if j == 0:
                            dve.wait_ge(C_ready, GS + 1)
                        state = state0[:, p, j, :]
                        nc.vector.tensor_tensor(state, state, C_all[:, p, :], ALU.mult).then_inc(weighted[j], 1)

                    scan(0)
                    scan(1)
                    weigh(0)
                    scan(2)
                    weigh(1)
                    weigh(2)
                    if first and p == 0 and i > 0 and closes(i - 1):
                        collect0(b, i - 1)
                    if isinstance(it, int):
                        step(b, i, it * 2 + p)

            def collect0(b, i):
                for j in range(J):
                    dve.wait_ge(summed[j], b * (K * N) + (i + 1) * N)
                    if i < 2:
                        dve.wait_ge(S["yinit"], at("yinit", (0, j), b))
                    else:
                        before = max(q for q in range(i) if closes(q))
                        dve.wait_ge(S["yev"], at("yev", (0, before, j), b))
                    acc = yacc0[:, j, :, :].rearrange("p h t -> p (h t)")
                    for dst, src in zip(lines(y[:, j, :], SCANS[i][1]), stored(acc)):
                        nc.vector.tensor_tensor(dst, dst, src, ALU.add).then_inc(S["yev"], note("yev", (0, i, j)))

            def scans0(b):
                first_rest(b, 0, 0)
                third_part(b, 0, 0)
                for j in range(J):
                    prepare_dt(b, 0, 0, j)
                for i in range(K):
                    for lo, hi in PIECES:
                        if hi - lo == 1:
                            pair0(b, i, lo, lo == 0)
                        else:
                            with dve.Fori(lo, hi) as it:
                                pair0(b, i, it, False)
                            step(b, i, 2 * hi - 1)
                collect0(b, K - 1)

            def weigh1(b, j, G, GS, slot, start):
                dve.wait_ge(hsum_ready, G * 4)
                dve.wait_ge(C_ready, GS)
                if not start:
                    dve.wait_ge(summed1, G - 1)
                nc.vector.tensor_tensor(yc1[:, slot, :], hsum[:, slot, :, :].rearrange("p h t -> p (h t)"),
                                        C_all[:, slot, :], ALU.mult).then_inc(weighted1, 1)

            def pair1(b, j, it, first, end):
                for p in range(2):
                    G = b * (J * N) + j * N + it * 2 + p
                    GS = b * NB_SPREAD + (K * N + j * N) + it * 2 + p

                    def scan(q):
                        dve.wait_ge(decay1_ready, G * 2 + (1 + q // 2))
                        state, decay = state1[:, p, q, :], decay1[:, p, q // 2, :]
                        if q % 2:
                            state, decay = state[:, ::-1], decay[:, ::-1]
                        nc.vector.tensor_tensor_scan(state, decay, state, 0.0, ALU.mult, ALU.add).then_inc(scanned1, 1)

                    dve.wait_ge(pool1_ready, G * 3 + 1)
                    scan(0)
                    dve.wait_ge(pool1_ready, G * 3 + 2)
                    scan(1)
                    dve.wait_ge(gate1_ready, G * 4 + 3)
                    dve.wait_ge(src1_ready, G + 1)
                    state = state1[:, p, 2, :].rearrange("p (c r) -> p c r", c=SIDE)
                    nc.vector.tensor_tensor(state, state, src1[:, p, :].rearrange("p (r c) -> p c r", r=SIDE),
                                            ALU.mult).then_inc(dve1_ready, 1)
                    if not (first and p == 0):
                        weigh1(b, j, G, GS, 1 - p, j == 0 and first)
                    dve.wait_ge(dve1_ready, G + 1)
                    scan(2)
                    dve.wait_ge(pool1_ready, G * 3 + 3)
                    scan(3)

            def sums_of_steps(b, j):
                dve.wait_ge(S["dl"], at("dl", (1, 0, J - 1 if j == 1 else j), b))
                if j > 0:
                    dve.wait_ge(S["cs"], at("cs", (j - 1, Q - 1), b))
                nc.vector.tensor_copy(delta_cols.rearrange("p (c r) -> p c r", c=SIDE),
                                      delta1[:, j, :].rearrange("p (r c) -> p c r", r=SIDE)).then_inc(
                    S["dc"], note("dc", j))
                dve.wait_ge(S["dc"], at("dc", j, b))
                for q in range(Q):
                    src, dst = delta1[:, j, :] if q < 2 else delta_cols, csum[j % 2][:, q, :]
                    if q % 2:
                        src, dst = src[:, ::-1], dst[:, ::-1]
                    nc.vector.tensor_tensor_scan(dst, one[:, :].broadcast_to([P, T]), src, 0.0,
                                                 ALU.mult, ALU.add).then_inc(S["cs"], note("cs", (j, q)))

            def scans1(b):
                first_rest(b, 1, 0)
                third_part(b, 1, 0)
                for j in range(J):
                    prepare_dt(b, 1, 0, j)
                sums_of_steps(b, 0)
                for j in range(J):
                    pair1(b, j, 0, True, False)
                    with dve.Fori(1, PAIRS - 1) as it:
                        pair1(b, j, it, False, False)
                    if j < J - 1:
                        sums_of_steps(b, j + 1)
                    pair1(b, j, PAIRS - 1, False, True)
                    G = b * (J * N) + (j + 1) * N
                    weigh1(b, j, G, b * NB_SPREAD + (K * N + (j + 1) * N), 1, False)
                    dve.wait_ge(summed1, G)
                    dve.wait_ge(S["yinit"], at("yinit", (1, j), b))
                    nc.vector.tensor_tensor(y[:, j, :], y[:, j, :], yacc1[:, :, :].rearrange("p h t -> p (h t)"),
                                            ALU.add).then_inc(S["yev"], note("yev", (1, j)))

            def tail(b, l):
                dve.wait_ge(S["ev"], at("ev", ("mu", l, 1), b))
                for j in range(J):
                    nc.vector.tensor_tensor(y[:, j, :], y[:, j, :], mu[:, :], ALU.subtract).then_inc(
                        S["cen"], note("cen", (l, j)))
                dve.wait_ge(S["rs"], at("rs", (l, 1), b))
                for j in range(J):
                    nc.vector.tensor_tensor(y[:, j, :], y[:, j, :], rs[:, :], ALU.mult).then_inc(
                        S["nrm"], note("nrm", (l, j)))
                for j in range(J):
                    dve.wait_ge(S["aff"], at("aff", (l, j), b))
                    nc.vector.tensor_tensor(y[:, j, :], y[:, j, :], gate[:, j, :], ALU.mult).then_inc(
                        S["gat"], note("gat", (l, j)))
                for c in range(2):
                    dve.wait_ge(S["ev"], at("ev", ("out", l, c, 1), b))
                    nc.vector.tensor_tensor(xT[:, c, :], xT[:, c, :], o2[:, c, :], ALU.add).then_inc(
                        S["res"], note("res", (l, c)))

            dve.wait_ge(loaded, 16 * LOADS)
            nc.vector.memset(one[:, :], 1.0).then_inc(setup, 1)
            nc.vector.tensor_copy(pick_row[:, :], pick_f[:, :]).then_inc(setup, 1)
            nc.vector.tensor_reduce(skip[:, 0, :], dk[:, :, :], mybir.AxisListType.X, ALU.add).then_inc(setup, 1)
            nc.vector.tensor_scalar(skip[:, 1, :], skip[:, 1, :], float(Q), None, ALU.mult).then_inc(setup, 1)
            dve.wait_ge(exp_a, 2)
            nc.vector.tensor_scalar(a0[:, :], a0[:, :], -1.0, None, ALU.mult).then_inc(setup, 1)
            nc.vector.tensor_scalar(a1[:, :], a1[:, :], -1.0, None, ALU.mult).then_inc(setup, 1)
            dve.wait_ge(setup, 6)
            with dve.Fori(0, NB) as b:
                front(b, 0)
                scans0(b)
                tail(b, 0)
                front(b, 1)
                scans1(b)
                tail(b, 1)


def kernel(**inputs):
    import numpy as np
    import concourse.bacc as bacc
    from concourse.bass_utils import run_bass_kernel_spmd

    v = {k: np.asarray(a) for k, a in inputs.items()}
    L0, L1 = "L0_conv_", "L1_conv_"

    def channels(a):
        return np.moveaxis(a.reshape(J, P, *a.shape[1:]), 0, 1)

    def three(w):
        return channels(np.concatenate([w[:, R:]] * 3 + [w[:, :R]], axis=1))

    group = np.zeros((CH, CH), np.float32)
    size = C // 32
    for g in range(CH // size):
        group[g * size:(g + 1) * size, g * size:(g + 1) * size] = 1.0 / size
    arrays = {
        "x": v["x"].reshape(-1, T, C).transpose(0, 2, 1),
        "w_in": np.stack([v[L0 + "W_in"].T, v[L1 + "W_in"]]),
        "conv_w": np.stack([channels(v[l + "conv_w"].reshape(DI, 9)) for l in (L0, L1)], axis=1),
        "conv_b": np.stack([channels(v[l + "conv_b"]) for l in (L0, L1)], axis=1),
        "w_x0": np.stack([three(v[L0 + "x_proj_weight"][k].T) for k in range(K)]),
        "w_dt0": v[L0 + "dt_projs_weight"].transpose(0, 2, 1),
        "dt_b0": np.stack([channels(v[L0 + "dt_projs_bias"][k]) for k in range(K)], axis=1),
        "a_log0": v[L0 + "A_logs"].reshape(K, J, P, N).transpose(2, 0, 1, 3).reshape(P, K * J * N),
        "d0": v[L0 + "Ds"].reshape(K, J, P).transpose(2, 1, 0),
        "w_x1": three(v[L1 + "W_x"]),
        "w_dt1": v[L1 + "W_dt"],
        "dt_b1": channels(v[L1 + "b_dt"]),
        "a_log1": channels(v[L1 + "A_log"]).reshape(P, J * N),
        "d1": channels(v[L1 + "D_param"]),
        "ln_w": np.stack([channels(v[L0 + "ln_w"]), channels(v[L1 + "gamma"])], axis=1),
        "ln_b": np.stack([channels(v[L0 + "ln_b"]), channels(v[L1 + "beta"])], axis=1),
        "w_out": np.stack([v[L0 + "W_out"].T, v[L1 + "W_out"]]),
        "group_mean": group,
        "eye": np.eye(P, dtype=np.float32),
        "pick": np.tile(np.eye(2 * N, dtype=np.float32), (3, 1)),
        "mean_one": np.full((P, P), 1.0 / DI, np.float32),
    }
    arrays = {k: np.ascontiguousarray(a) for k, a in arrays.items()}

    def build(counts):
        nc = bacc.Bacc("TRN2", target_bir_lowering=False, num_devices=1)
        ins = {k: nc.dram_tensor("in_" + k, a.shape, mybir.dt.from_np(a.dtype), kind="ExternalInput").ap()
               for k, a in arrays.items()}
        out = nc.dram_tensor("out_x", arrays["x"].shape, F32, kind="ExternalOutput").ap()
        program(nc, counts, out=out, **ins)
        return nc

    first = Counts()
    build(first)
    nc = build(Counts(first))
    r = run_bass_kernel_spmd(nc, [{"in_" + k: a for k, a in arrays.items()}], core_ids=[0])
    y = np.asarray(r.results[0]["out_x"])
    return np.ascontiguousarray(y.transpose(0, 2, 1)).reshape(v["x"].shape)
```

```python
import concourse.bass as bass
from concourse import mybir
from contextlib import ExitStack

F32 = mybir.dt.float32
BF16 = mybir.dt.bfloat16
ALU = mybir.AluOpType
ACT = mybir.ActivationFunctionType

P = 128
NB, SIDE, C, DI, N, R, K = 8, 32, 192, 384, 16, 12, 8
T = SIDE * SIDE
HT = T // 2
CH = C // 2
J = DI // P
XR = 6 * N
PAD = SIDE + 2
PAIRS = N // 2
QUADS = N // 4
Q = 4

SCANS = [(0, "rows", False), (4, "rows", True), (3, "mirror", False), (7, "mirror", True),
         (1, "cols", False), (5, "cols", True), (2, "cols", True), (6, "cols", False)]
PIECES = [(0, 1), (1, 4), (4, 5), (5, 6), (6, 7), (7, 8)]
LN_1E12 = 27.631021115928547


def opens(i):
    return i == 0 or SCANS[i][1] != SCANS[i - 1][1]


def closes(i):
    return i == K - 1 or SCANS[i][1] != SCANS[i + 1][1]


def lines(ap, order):
    if order == "cols":
        v = ap.rearrange("p (r i two) -> p two i r", r=SIDE, two=2)
    else:
        v = ap.rearrange("p (i two c) -> p two i c", two=2, c=SIDE)
    if order == "mirror":
        return v[:, 0, :, ::-1], v[:, 1, :, :]
    return v[:, 0, :, :], v[:, 1, :, ::-1]


def stored(ap):
    v = ap.rearrange("p (i two c) -> p two i c", two=2, c=SIDE)
    return v[:, 0, :, :], v[:, 1, :, :]


class Counts:

    def __init__(self, known=None):
        self.known, self.now, self.marks = known, {}, {}

    def note(self, kind, step, by=1):
        self.now[kind] = self.now.get(kind, 0) + by
        self.marks[kind, step] = self.now[kind]
        return by

    def at(self, kind, step, b):
        if self.known is None:
            return 1
        return b * self.known.now[kind] + self.known.marks[kind, step]


def program(nc, counts, x, out, w_in, conv_w, conv_b, w_x0, w_dt0, dt_b0, a_log0, d0,
            w_x1, w_dt1, dt_b1, a_log1, d1, ln_w, ln_b, w_out, group_mean, eye, pick, mean_one):
    ctx = ExitStack()
    with ctx:
        def sb(name, shape, dt=F32):
            return ctx.enter_context(nc.sbuf_tensor(name, shape, dt))

        def semaphore(name):
            return ctx.enter_context(nc.semaphore(name))

        identity = sb("identity", [P, P])
        mean_ones = sb("mean_ones", [P, P])
        groups = sb("groups", [CH, CH])
        pick_f = sb("pick_f", [XR, 2 * N])
        pick_row = sb("pick_row", [XR, 2 * N], BF16)
        one = sb("one", [P, 1])
        cw = sb("cw", [P, 2, J, 9])
        cb = sb("cb", [P, 2, J])
        wx = sb("wx", [P, 2, J, XR + R])
        wdt = sb("wdt", [XR + R, 2, DI])
        wx1 = sb("wx1", [P, J, XR + R])
        wdt1 = sb("wdt1", [XR + R, DI])
        dtb0 = sb("dtb0", [P, K, J])
        dtb1 = sb("dtb1", [P, J])
        a0 = sb("a0", [P, K * J * N])
        a1 = sb("a1", [P, J * N])
        a1_now = sb("a1_now", [P, 2])
        dk = sb("dk", [P, J, K])
        skip = sb("skip", [P, 2, J])
        lnw = sb("lnw", [P, 2, J])
        lnb = sb("lnb", [P, 2, J])
        xT = sb("xT", [CH, 2, T])
        u = sb("u", [P, J, T])
        y = sb("y", [P, J, T])
        B_all = sb("B_all", [P, 2, T])
        C_all = sb("C_all", [P, 2, T])
        parts = sb("parts", [XR, 2, T], BF16)
        xdbl = sb("xdbl", [XR + R, T])
        stats = sb("stats", [CH, 2, 2, 6])
        mv = sb("mv", [CH, 2, 2])
        sq2 = sb("sq2", [CH, 2])
        gs = sb("gs", [CH, 2, 2])
        gvar = sb("gvar", [CH, 2])
        rstd = sb("rstd", [CH, 2])
        room = sb("room", [P, 34, T])

        def by_parity(lo):
            return room[:, lo:lo + 2 * J, :].rearrange("p (s j) t -> p s j t", s=2)

        delta0 = by_parity(0)
        du0 = by_parity(6)
        decay0 = by_parity(16)
        source0 = by_parity(22)
        state0 = by_parity(28)
        delta1 = room[:, 0:3, :]
        e1 = room[:, 3:6, :]
        du1 = u
        csum = [room[:, 6:10, :], room[:, 26:30, :]]
        decay1 = [(room[:, a, :], room[:, c, :]) for a, c in ((10, 11), (12, 13), (3, 4), (5, 33))]
        src1 = room[:, 14:16, :]
        state1 = room[:, 16:24, :].rearrange("p (s q) t -> p s q t", s=2)
        yc1 = room[:, 24:26, :]
        delta_cols = room[:, 30, :]
        soft = [room[:, 12:16, :], room[:, 26:30, :]]
        xz = [room[0:CH, 0:2, :], room[0:CH, 26:28, :]]
        gate = [room[:, 6:9, :], room[:, 28:31, :]]
        w_z = [room[0:CH, 12, 0:2 * DI].rearrange("p (h m) -> p h m", h=2),
               room[0:CH, 31, 0:2 * DI].rearrange("p (h m) -> p h m", h=2)]
        wout = [room[:, 13, 0:J * C].rearrange("p (j c) -> p j c", j=J),
                room[:, 32, 0:J * C].rearrange("p (j c) -> p j c", j=J)]
        win = room[0:CH, 0, 0:2 * DI].rearrange("p (h m) -> p h m", h=2)
        taps = room[:, 3:5, :].rearrange("p a t -> p (a t)")[:, 0:9 * P].rearrange("p (k m) -> p k m", m=P)
        xn = room[0:CH, 17:19, :]
        padded = room[:, 20:24, :].rearrange("p a t -> p (a t)")[:, 0:J * PAD * PAD].rearrange(
            "p (j r c) -> p j r c", j=J, r=PAD)
        mu = room[:, 20, :]
        rs = room[:, 21, :]
        sq = room[:, 22:25, :]
        o2 = room[0:CH, 17:19, :]

        bank = ctx.enter_context(nc.psum_tensor("bank", [P, 8, HT], F32))
        WORK = (6, 7)
        SPARE = (4, 5)
        yacc0 = bank[:, 0:6, :].rearrange("p (j h) t -> p j h t", j=J)
        yacc1 = bank[:, 0:2, :]
        hsum = bank[:, 2:6, :].rearrange("p (s h) t -> p s h t", s=2)

        names = ["load_wx0", "load_wx1", "load_win1", "load_wz0", "load_wz1", "load_wout0", "load_wout1",
                 "xz", "silu", "mm", "ev", "stat", "gs", "xn", "pad", "conv", "u",
                 "p1", "r1", "p2", "parts", "ab", "ab_first", "ex", "ln", "d", "g1", "g", "dl", "du",
                 "yinit", "yev", "cs", "dc", "cen", "sq", "rs", "nrm", "aff", "gat", "res"]
        S = {n: semaphore("s_" + n) for n in names}
        note, at = counts.note, counts.at
        setup = semaphore("setup")
        loaded = semaphore("loaded")
        exp_a = semaphore("exp_a")
        load_x_done = semaphore("load_x_done")
        store_done = semaphore("store_done")
        decay_ready = [semaphore(f"decay_ready_tile{j}") for j in range(J)]
        source_ready = [semaphore(f"source_ready_tile{j}") for j in range(J)]
        scanned = [semaphore(f"scanned_tile{j}") for j in range(J)]
        weighted = [semaphore(f"weighted_tile{j}") for j in range(J)]
        summed = [semaphore(f"summed_tile{j}") for j in range(J)]
        B_spread = semaphore("B_spread")
        C_spread = semaphore("C_spread")
        B_ready = semaphore("B_ready")
        C_ready = semaphore("C_ready")
        taps_ready = semaphore("taps_ready")
        win0_loaded = semaphore("win0_loaded")
        a1_ready = semaphore("a1_ready")
        decay1_ready = semaphore("decay1_ready")
        gate1_ready = semaphore("gate1_ready")
        src1_ready = semaphore("src1_ready")
        pool1_ready = semaphore("pool1_ready")
        dve1_ready = semaphore("dve1_ready")
        scanned1 = semaphore("scanned1")
        hsum_ready = semaphore("hsum_ready")
        weighted1 = semaphore("weighted1")
        summed1 = semaphore("summed1")
        NB_SPREAD = K * N + J * N

        def halves(h):
            return slice(h * HT, (h + 1) * HT)

        block = ctx.enter_context(nc.Block())
        LOADS = 16

        @block.sync
        def _(sp):
            def load(dst, src):
                sp.dma_start(dst, src).then_inc(loaded, 16)

            load(groups[:, :], group_mean)
            load(identity[:, :], eye)
            load(pick_f[:, :], pick)
            load(dtb0[:, :, :], dt_b0)
            load(dtb1[:, :], dt_b1)
            load(a0[:, :], a_log0)
            load(a1[:, :], a_log1)
            load(dk[:, :, :], d0)
            load(skip[:, 1, :], d1)
            load(cw[:, :, :, :], conv_w)
            load(cb[:, :, :], conv_b)
            load(lnw[:, :, :], ln_w)
            load(lnb[:, :, :], ln_b)
            load(wx1[:, :, :], w_x1)
            load(wdt1[XR:XR + R, :], w_dt1)
            load(mean_ones[:, :], mean_one)
            def load_x(b):
                src = x[slice(b, b + 1) if isinstance(b, int) else bass.ds(b, 1), :, :]
                sp.dma_start(xT[:, :, :], src.rearrange("o (h p) t -> p (o h) t", p=CH)).then_inc(load_x_done, 16)

            def load_win(l, sem, by=16):
                sp.dma_start(win, w_in[l, :, 0:DI].rearrange("(h p) m -> p h m", p=CH)).then_inc(sem, by)

            def load_wz(l):
                kind = f"load_wz{l}"
                sp.dma_start(w_z[l], w_in[l, :, DI:2 * DI].rearrange("(h p) m -> p h m", p=CH)).then_inc(
                    S[kind], note(kind, 0, 16))

            def load_wout(l):
                kind = f"load_wout{l}"
                sp.dma_start(wout[l], w_out[l].rearrange("(j p) c -> p j c", p=P)).then_inc(S[kind], note(kind, 0, 16))

            def image(b, more):
                for i, (k, _, _) in enumerate(SCANS):
                    if i >= 2:
                        sp.wait_ge(S["ev"], at("ev", ("dt", 0, i - 2, J - 1, 1), b))
                    slot = f"load_wx{i % 2}"
                    sp.dma_start(wx[:, i % 2, :, :], w_x0[k]).then_inc(S[slot], note(slot, i, 16))
                    sp.dma_start(wdt[XR:XR + R, i % 2, :], w_dt0[k]).then_inc(S[slot], note(slot, i, 16))
                sp.wait_ge(S["dl"], at("dl", (0, K - 1, J - 1), b))
                load_wz(0)
                load_wout(0)
                sp.wait_ge(S["yev"], at("yev", (0, K - 1, J - 1), b))
                load_win(1, S["load_win1"], note("load_win1", 0, 16))
                load_wz(1)
                load_wout(1)
                sp.wait_ge(S["yev"], at("yev", (1, J - 1), b))
                if more:
                    load_win(0, win0_loaded)
                sp.wait_ge(S["res"], at("res", (1, 1), b))
                dst = out[slice(b, b + 1) if isinstance(b, int) else bass.ds(b, 1), :, :]
                sp.dma_start(dst.rearrange("o (h p) t -> p (o h) t", p=CH), xT[:, :, :]).then_inc(store_done, 16)
                sp.wait_ge(store_done, b * 16 + 16)

            load_x(0)
            load_win(0, win0_loaded)
            before = dict(counts.now)
            if NB > 1:
                with sp.Fori(0, NB - 1) as b:
                    image(b, True)
                    load_x(b + 1)
            counts.now = before
            image(NB - 1, False)

        @block.tensor
        def _(pe):
            last = {}

            def work(b, h, step, waits, products, rows=P, cols=HT):
                free = last[h](b) if last[h] else None
                ev_waits = [w for w in waits if w[0] == "ev"]
                if free and not (ev_waits and free[0] is S["ev"]):
                    pe.wait_ge(*free)
                for kind, s in waits:
                    pe.wait_ge(S[kind], at(kind, s, b))
                for i, (lhsT, rhs) in enumerate(products):
                    ins = nc.tensor.matmul(bank[0:rows, WORK[h], 0:cols], lhsT, rhs,
                                           start=(i == 0), stop=(i == len(products) - 1))
                ins.then_inc(S["mm"], note("mm", step))
                last[h] = lambda b, step=step: (S["ev"], at("ev", step, b))

            def front(b, l):
                work(b, 0, ("gn", l), [("stat", (l, "msq"))],
                     [(groups[:, :], mv[:, :, :].rearrange("p h s -> p (h s)"))], rows=CH, cols=4)
                if l == 0:
                    pe.wait_ge(win0_loaded, b * 16 + 16)
                else:
                    pe.wait_ge(S["load_win1"], at("load_win1", 0, b))
                for m in range(J):
                    for h in range(2):
                        work(b, h, ("in", l, m, h), [("xn", (l, 1))],
                             [(win[:, c, m * P:(m + 1) * P], xn[:, c, halves(h)]) for c in range(2)])
                pe.wait_ge(taps_ready, b * 2 + (l + 1))
                pe.wait_ge(S["pad"], at("pad", l, b))
                for h in range(2):
                    r0 = h * (SIDE // 2)
                    work(b, h, ("conv", l, h), [("ev", ("in", l, J - 1, 1))],
                         [(taps[:, t, :],
                           padded[:, J - 1, r0 + t // 3:r0 + t // 3 + SIDE // 2, t % 3:t % 3 + SIDE])
                          for t in range(9)])

            def gate_projection(b, l, j):
                if j == 0:
                    pe.wait_ge(S[f"load_wz{l}"], at(f"load_wz{l}", 0, b))
                for h in range(2):
                    work(b, h, ("z", l, j, h), [("xz", (l, 1))],
                         [(w_z[l][:, c, j * P:(j + 1) * P], xz[l][:, c, halves(h)]) for c in range(2)])

            def prepare_bc(b, l, i):
                if l == 1:
                    for h in range(2):
                        work(b, h, ("xd", 1, 0, h), [("u", (1, J - 2)), ("ev", ("conv", 1, 1))],
                             [(wx1[:, j, :], u[:, j, halves(h)]) for j in range(J)], rows=XR + R)
                    return
                if i == 0:
                    pe.wait_ge(S["u"], at("u", (0, J - 2), b))
                    pe.wait_ge(S["ev"], at("ev", ("conv", 0, 1), b))
                pe.wait_ge(S[f"load_wx{i % 2}"], at(f"load_wx{i % 2}", i, b))
                eighth = SIDE // 4
                for h in range(2):
                    pe.wait_ge(*last[h](b))
                    dst = stored(bank[0:XR + R, WORK[h], :])
                    for line in range(2):
                        for j in range(J):
                            rhs = lines(u[:, j, :], SCANS[i][1])[line][:, h * eighth:(h + 1) * eighth, :]
                            ins = nc.tensor.matmul(dst[line], wx[:, i % 2, j, :], rhs,
                                                   start=(j == 0), stop=(j == J - 1))
                    ins.then_inc(S["mm"], note("mm", ("xd", 0, i, h)))
                    last[h] = lambda b, step=("xd", 0, i, h): (S["ev"], at("ev", step, b))

            def prepare_dt(b, l, i, j):
                w = wdt[XR:XR + R, i % 2, :] if l == 0 else wdt1[XR:XR + R, :]
                for h in range(2):
                    work(b, h, ("dt", l, i, j, h), [("ev", ("xd", l, i, h))] if l == 0 and i > 0 and j == 0 else [],
                         [(w[:, j * P:(j + 1) * P], xdbl[XR:XR + R, halves(h)])])

            def spread(row, par, sem):
                for h in range(2):
                    ins = nc.tensor.matmul(bank[:, WORK[h], :], pick_row[:, row].broadcast_to([XR, P]),
                                           parts[:, par, halves(h)], start=True, stop=True)
                ins.then_inc(sem, 1)

            def add_state(b, G, j, p, start, stop):
                for h in range(2):
                    ins = nc.tensor.matmul(yacc0[:, j, h, :], identity[:, :], state0[:, p, j, halves(h)],
                                           start=start, stop=stop)
                ins.then_inc(summed[j], 1)

            def step(b, i, n):
                if n not in (0, 8, 9, 10) or (i == K - 1 and n == 0):
                    return None
                done = b * NB_SPREAD + (i * N + n + 3)
                for h in range(2):
                    last[h] = lambda b, v=done: (B_ready, v)
                if i == K - 1:
                    j = n - 8
                    gate_projection(b, 0, j)
                    return "z", 0, j, 1
                if n == 0:
                    prepare_bc(b, 0, i + 1)
                    return "xd", 0, i + 1, 1
                j = n - 8
                prepare_dt(b, 0, i + 1, j)
                return "dt", 0, i + 1, j, 1

            def pair0(b, i, it, prepared=None):
                for p in range(2):
                    n = it * 2 + p
                    static = isinstance(n, int)
                    G = b * (K * N) + i * N + it * 2 + p
                    GS = b * NB_SPREAD + i * N + it * 2 + p

                    def spread_ahead(lead, row0, signal):
                        par, row = i % 2, n + lead
                        if static and row >= N:
                            par, row = (i + 1) % 2, row - N
                        row = row + row0
                        spread(slice(row, row + 1) if static else bass.ds(row, 1), par, signal)

                    def add(j):
                        start, stop = static and n == 0 and opens(i), static and n == N - 1 and closes(i)
                        if start and i > 0:
                            pe.wait_ge(S["yev"], at("yev", (0, i - 1, j), b))
                        pe.wait_ge(weighted[j], G + 1)
                        add_state(b, G, j, p, start, stop)

                    final = static and i == K - 1
                    if not (final and n == N - 1):
                        if prepared:
                            pe.wait_ge(S["ev"], at("ev", prepared, b))
                        pe.wait_ge(B_ready, GS + 2)
                        spread_ahead(1, N, C_spread)
                    add(0)
                    if not (final and n >= N - 2):
                        if static and n == N - 2:
                            pe.wait_ge(S["parts"], at("parts", (0, i + 1), b))
                        pe.wait_ge(C_ready, GS + 2)
                        spread_ahead(2, 0, B_spread)
                    add(1)
                    if p == 1 or static:
                        prepared = None
                    if static:
                        prepared = step(b, i, n)
                    add(2)
                return prepared

            def scans0(b):
                prepare_bc(b, 0, 0)
                for j in range(J):
                    prepare_dt(b, 0, 0, j)
                pe.wait_ge(S["parts"], at("parts", (0, 0), b))
                GS = b * NB_SPREAD
                pe.wait_ge(*last[1](b))
                spread(slice(0, 1), 0, B_spread)
                pe.wait_ge(B_ready, GS + 1)
                spread(slice(N, N + 1), 0, C_spread)
                pe.wait_ge(C_ready, GS + 1)
                spread(slice(1, 2), 0, B_spread)
                for i in range(K):
                    prepared = None
                    for lo, hi in PIECES:
                        if hi - lo == 1:
                            prepared = pair0(b, i, lo, prepared)
                        else:
                            with pe.Fori(lo, hi) as it:
                                pair0(b, i, it)

            def quad1(b, j, it, first, end):
                for m in range(4):
                    p = m % 2
                    n = it * 4 + m
                    G = b * (J * N) + j * N + it * 4 + m
                    GS = b * NB_SPREAD + (K * N + j * N) + it * 4 + m
                    fresh = j == 0 and first and m < 2
                    last_pair = j == J - 1 and end and m >= 2
                    if last_pair and p == 1:
                        pe.wait_ge(C_ready, GS)
                    else:
                        pe.wait_ge(B_ready, GS + 2)
                    row = n + N
                    spread(slice(row, row + 1) if isinstance(row, int) else bass.ds(row, 1), 0, C_spread)
                    if not fresh:
                        pe.wait_ge(weighted1, G - 1)

                    def add_direction(q):
                        pe.wait_ge(scanned1, G * 4 + (q + 1))
                        for h in range(2):
                            if q < 2:
                                rhs = state1[:, p, q, halves(h)]
                            else:
                                rhs = state1[:, p, q, :].rearrange("p (c r) -> p r c", c=SIDE)[
                                    :, h * (SIDE // 2):(h + 1) * (SIDE // 2), :]
                            ins = nc.tensor.matmul(hsum[:, p, h, :], identity[:, :], rhs,
                                                   start=(q == 0), stop=(q == Q - 1))
                        ins.then_inc(hsum_ready, 1)

                    add_direction(0)
                    add_direction(1)
                    if not last_pair:
                        pe.wait_ge(C_ready, GS + 1)
                        row = p if end and m >= 2 else n + 2
                        spread(slice(row, row + 1) if isinstance(row, int) else bass.ds(row, 1), 0, B_spread)
                    if not (first and m == 0):
                        add_weighted(b, j, G, 1 - p, first and m == 1, False)
                    add_direction(2)
                    add_direction(3)

            def add_weighted(b, j, G, slot, start, stop):
                if start and j > 0:
                    pe.wait_ge(S["yev"], at("yev", (1, j - 1), b))
                pe.wait_ge(weighted1, G)
                for h in range(2):
                    ins = nc.tensor.matmul(yacc1[:, h, :], identity[:, :], yc1[:, slot, halves(h)],
                                           start=start, stop=stop)
                ins.then_inc(summed1, 1)

            def scans1(b):
                prepare_bc(b, 1, 0)
                for j in range(J):
                    prepare_dt(b, 1, 0, j)
                pe.wait_ge(S["parts"], at("parts", (1, 0), b))
                pe.wait_ge(*last[1](b))
                spread(slice(0, 1), 0, B_spread)
                pe.wait_ge(B_ready, b * NB_SPREAD + (K * N + 1))
                spread(slice(1, 2), 0, B_spread)
                for j in range(J):
                    quad1(b, j, 0, True, False)
                    with pe.Fori(1, QUADS - 1) as it:
                        quad1(b, j, it, False, False)
                    quad1(b, j, QUADS - 1, False, True)
                    if j == J - 1:
                        for h in range(2):
                            last[h] = lambda b: (C_ready, b * NB_SPREAD + NB_SPREAD)
                        gate_projection(b, 1, 0)
                    add_weighted(b, j, b * (J * N) + (j + 1) * N, 1, False, True)

            def tail(b, l):
                def over_tiles(kind, step, products):
                    pe.wait_ge(*last[1](b))
                    for j in range(J):
                        pe.wait_ge(S[kind], at(kind, step(j), b))
                        for name, banks, rows, lhsT, rhs in products:
                            for h in range(2):
                                ins = nc.tensor.matmul(bank[0:rows, banks[h], :], lhsT(j), rhs[:, j, halves(h)],
                                                       start=(j == 0), stop=(j == J - 1))
                            if j == J - 1:
                                ins.then_inc(S["mm"], note("mm", name))
                    for h in range(2):
                        last[h] = lambda b, name=products[0][0]: (S["ev"], at("ev", name, b))

                over_tiles("yev", lambda j: (0, K - 1, j) if l == 0 else (1, j),
                           [(("mu", l), WORK, P, lambda j: mean_ones[:, :], y)])
                if l == 1:
                    gate_projection(b, 1, 1)
                    gate_projection(b, 1, 2)
                over_tiles("sq", lambda j: (l, j),
                           [(("var", l), WORK, P, lambda j: mean_ones[:, :], sq)])
                pe.wait_ge(S[f"load_wout{l}"], at(f"load_wout{l}", 0, b))
                over_tiles("gat", lambda j: (l, j),
                           [(("out", l, c), banks, CH, lambda j, c=c: wout[l][:, j, c * CH:(c + 1) * CH], y)
                            for c, banks in ((0, WORK), (1, SPARE))])

            pe.wait_ge(loaded, 16 * LOADS)
            pe.wait_ge(setup, 6)
            with pe.Fori(0, NB) as b:
                for h in range(2):
                    last[h] = None
                front(b, 0)
                scans0(b)
                for h in range(2):
                    last[h] = lambda b: (C_ready, b * NB_SPREAD + K * N)
                tail(b, 0)
                front(b, 1)
                scans1(b)
                tail(b, 1)

        @block.scalar
        def _(act):
            def take(b, step, dst, h, func=ACT.Copy, rows=P, cols=HT, src=None, **kw):
                act.wait_ge(S["mm"], at("mm", step, b))
                nc.scalar.activation(dst, bank[0:rows, WORK[h], 0:cols] if src is None else src, func,
                                     **kw).then_inc(S["ev"], note("ev", step))

            def front(b, l):
                take(b, ("gn", l), gs[:, :, :].rearrange("p h s -> p (h s)"), 0, rows=CH, cols=4)
                act.wait_ge(S["stat"], at("stat", (l, "gvar"), b))
                nc.scalar.activation(rstd[:, :], gvar[:, :], ACT.Ln, bias=1e-5).then_inc(
                    S["gs"], note("gs", (l, "ln")))
                act.wait_ge(S["gs"], at("gs", (l, "ln"), b))
                nc.scalar.activation(rstd[:, :], rstd[:, :], ACT.Exp, scale=-0.5).then_inc(
                    S["gs"], note("gs", (l, "rstd")))
                act.wait_ge(S["xn"], at("xn", (l, 1), b))
                for m in range(J):
                    for h in range(2):
                        rows = slice(1 + h * (SIDE // 2), 1 + (h + 1) * (SIDE // 2))
                        take(b, ("in", l, m, h), padded[:, m, rows, 1:1 + SIDE], h,
                             src=bank[:, WORK[h], :].rearrange("p (r c) -> p r c", c=SIDE))
                for h in range(2):
                    take(b, ("conv", l, h), u[:, J - 1, halves(h)], h, func=ACT.Silu, bias=cb[:, l, J - 1:J])
                for j in range(J - 1):
                    act.wait_ge(S["conv"], at("conv", (l, j, 8), b))
                    nc.scalar.activation(u[:, j, :], u[:, j, :], ACT.Silu).then_inc(S["u"], note("u", (l, j)))

            def prepare_bc(b, l, i):
                for h in range(2):
                    take(b, ("xd", l, i, h), xdbl[:, halves(h)], h, rows=XR + R)
                slot = parts[:, i % 2, :]
                act.wait_ge(S["ev"], at("ev", ("xd", l, i, 1), b))
                nc.scalar.activation(slot[:, :], xdbl[0:XR, :], ACT.Copy).then_inc(S["p1"], note("p1", (l, i)))

            def second_part(b, l, i):
                slot = parts[:, i % 2, :]
                act.wait_ge(S["r1"], at("r1", (l, i), b))
                nc.scalar.activation(slot[32:64, :], xdbl[32:64, :], ACT.Copy).then_inc(S["p2"], note("p2", (l, i, 0)))
                nc.scalar.activation(slot[64:96, :], xdbl[64:96, :], ACT.Copy).then_inc(S["p2"], note("p2", (l, i)))

            def take_dt(b, l, i, j):
                delta = delta0[:, i % 2, j, :] if l == 0 else delta1[:, j, :]
                bias = dtb0[:, SCANS[i][0], j:j + 1] if l == 0 else dtb1[:, j:j + 1]
                for h in range(2):
                    take(b, ("dt", l, i, j, h), delta[:, halves(h)], h, func=ACT.Identity, bias=bias)

            def absolute(b, l, i, j):
                delta = delta0[:, i % 2, j, :] if l == 0 else delta1[:, j, :]
                e = du0[:, i % 2, j, :] if l == 0 else e1[:, j, :]
                act.wait_ge(S["ev"], at("ev", ("dt", l, i, j, 1), b))
                nc.scalar.activation(e, delta, ACT.Abs).then_inc(S["ab"], note("ab", (l, i, j)))

            def exponent(b, l, i, j):
                e = du0[:, i % 2, j, :] if l == 0 else e1[:, j, :]
                if i == 0:
                    act.wait_ge(S["ab_first"], at("ab_first", (l, j), b))
                else:
                    act.wait_ge(S["ab"], at("ab", (l, i, j), b))
                nc.scalar.activation(e, e, ACT.Exp, scale=-1.0).then_inc(S["ex"], note("ex", (l, i, j)))

            def logarithms(b, l, i):
                for j in range(J):
                    e = du0[:, i % 2, j, :] if l == 0 else e1[:, j, :]
                    act.wait_ge(S["ex"], at("ex", (l, i, j), b))
                    if j == 0 and i > 0:
                        act.wait_ge(S["dl"], at("dl", (l, i - 1, J - 1), b))
                    nc.scalar.activation(soft[l][:, j, :], e, ACT.Ln, bias=1.0).then_inc(
                        S["ln"], note("ln", (l, i, j)))

            def prepare_first(b, l):
                prepare_bc(b, l, 0)
                take_dt(b, l, 0, 0)
                for j in range(1, J):
                    take_dt(b, l, 0, j)
                    exponent(b, l, 0, j - 1)
                exponent(b, l, 0, J - 1)
                logarithms(b, l, 0)
                second_part(b, l, 0)

            def take_spread(GS, slot, sem_in, sem_out, dst):
                act.wait_ge(sem_in, GS + 1)
                nc.scalar.activation(dst[:, slot, :], bank[:, WORK[0]:WORK[1] + 1, :].rearrange("p h t -> p (h t)"),
                                     ACT.Copy).then_inc(sem_out, 1)

            def step(b, i, n):
                if i == K - 1:
                    if n in (9, 10, 11):
                        j = n - 9
                        for h in range(2):
                            take(b, ("z", 0, j, h), gate[0][:, j, halves(h)], h)
                    if n == N - 1:
                        act.wait_ge(S["ev"], at("ev", ("z", 0, J - 1, 1), b))
                        for j in range(J):
                            nc.scalar.activation(gate[0][:, j, :], gate[0][:, j, :], ACT.Silu).then_inc(
                                S["silu"], note("silu", (0, j)))
                    return
                i = i + 1
                if n == 1:
                    prepare_bc(b, 0, i)
                if n == 8:
                    second_part(b, 0, i)
                if n in (9, 10, 11):
                    take_dt(b, 0, i, n - 9)
                if n in (10, 11, 12):
                    exponent(b, 0, i, n - 10)
                if n in (9, 10, 11):
                    absolute(b, 0, i, n - 9)

            def decays(b, i, n, it, p, fresh, G, tiles=range(J)):
                for j in tiles:
                    if isinstance(n, int) and n == 0:
                        act.wait_ge(S["dl"], at("dl", (0, i, j), b))
                    if not fresh:
                        act.wait_ge(scanned[j], G - 1)
                    col = (SCANS[i][0] * J + j) * N + n
                    sel = slice(col, col + 1) if isinstance(col, int) else bass.ds(col, 1)
                    nc.scalar.activation(decay0[:, p, j, :], delta0[:, i % 2, j, :], ACT.Exp,
                                         scale=a0[:, sel]).then_inc(decay_ready[j], 1)

            def pair0(b, i, it):
                for p in range(2):
                    n = it * 2 + p
                    static = isinstance(n, int)
                    G = b * (K * N) + i * N + it * 2 + p
                    GS = b * NB_SPREAD + i * N + it * 2 + p
                    final = static and i == K - 1
                    if final and n == N - 1:
                        step(b, i, n)
                    if not (final and n == N - 1):
                        if static and n == N - 1:
                            decays(b, i + 1, 0, 0, 0, False, G + 1)
                        else:
                            decays(b, i, n + 1, it, 1 - p, static and i == 0 and n == 0, G + 1)
                    if static and not (final and n == N - 1):
                        step(b, i, n)
                    if not (final and n == N - 1):
                        if not (static and i == 0 and n == 0):
                            act.wait_ge(weighted[J - 1], G)
                        take_spread(GS + 1, 1 - p, C_spread, C_ready, C_all)
                    if not (final and n >= N - 2):
                        act.wait_ge(source_ready[J - 1], G + 1)
                        take_spread(GS + 2, p, B_spread, B_ready, B_all)
                    if static and n == 12 and i < K - 1:
                        logarithms(b, 0, i + 1)

            def scans0(b):
                prepare_first(b, 0)
                GS = b * NB_SPREAD
                decays(b, 0, 0, 0, 0, True, 0, [0])
                take_spread(GS, 0, B_spread, B_ready, B_all)
                decays(b, 0, 0, 0, 0, True, 0, [1])
                take_spread(GS, 0, C_spread, C_ready, C_all)
                decays(b, 0, 0, 0, 0, True, 0, [2])
                take_spread(GS + 1, 1, B_spread, B_ready, B_all)
                for i in range(K):
                    for lo, hi in PIECES:
                        if hi - lo == 1:
                            pair0(b, i, lo)
                        else:
                            with act.Fori(lo, hi) as it:
                                pair0(b, i, it)

            def quad1(b, j, it, first, end):
                for m in range(4):
                    p = m % 2
                    n = it * 4 + m
                    G = b * (J * N) + j * N + it * 4 + m
                    GS = b * NB_SPREAD + (K * N + j * N) + it * 4 + m
                    fresh = j == 0 and first and m < 2
                    if p == 0:
                        if not fresh:
                            act.wait_ge(gate1_ready, G * 4)
                        for k in range(2):
                            col = j * N + n + k
                            sel = slice(col, col + 1) if isinstance(col, int) else bass.ds(col, 1)
                            nc.scalar.activation(a1_now[:, k:k + 1], a1[:, sel], ACT.Copy).then_inc(a1_ready, 1)
                        act.wait_ge(a1_ready, G + 2)
                        if first and m == 0:
                            act.wait_ge(S["dl"], at("dl", (1, 0, j), b))
                        if first and m == 2 and j == 0:
                            act.wait_ge(S["dl"], at("dl", (1, 0, J - 1), b))
                        for k in range(2):
                            for o in range(2):
                                if not (j == 0 and first):
                                    act.wait_ge(scanned1, G * 4 + (4 * k - 16 + 2 * (o + 1)))
                                src = delta1[:, j, :]
                                dst = decay1[m + k][o]
                                if o == 1:
                                    src = src.rearrange("p (r c) -> p c r", r=SIDE)
                                    dst = dst.rearrange("p (c r) -> p c r", c=SIDE)
                                nc.scalar.activation(dst, src, ACT.Exp, scale=a1_now[:, k:k + 1]).then_inc(
                                    decay1_ready, 1)
                    if not (fresh and p == 0):
                        if not fresh:
                            act.wait_ge(weighted1, G - 2)
                        take_spread(GS - 1, 1 - p, C_spread, C_ready, C_all)
                    for q in range(Q):
                        if first and m == 0:
                            act.wait_ge(S["cs"], at("cs", (j, q), b))
                        if not fresh:
                            act.wait_ge(hsum_ready, G * 4 - (8 - (q + 1)))
                        nc.scalar.activation(state1[:, p, q, :], csum[j % 2][:, q, :], ACT.Sigmoid,
                                             scale=a1_now[:, p:p + 1], bias=LN_1E12).then_inc(gate1_ready, 1)
                    if not (j == J - 1 and end and m == 3):
                        if not (fresh and p == 0):
                            act.wait_ge(src1_ready, G)
                        take_spread(GS + 1, 1 - p, B_spread, B_ready, B_all)

            def scans1(b):
                prepare_first(b, 1)
                take_spread(b * NB_SPREAD + K * N, 0, B_spread, B_ready, B_all)
                for j in range(J):
                    quad1(b, j, 0, True, False)
                    with act.Fori(1, QUADS - 1) as it:
                        quad1(b, j, it, False, False)
                    quad1(b, j, QUADS - 1, False, True)
                act.wait_ge(weighted1, b * (J * N) + (J * N - 2))
                take_spread(b * NB_SPREAD + NB_SPREAD - 1, 1, C_spread, C_ready, C_all)

            def take_pair(b, step, dst, banks, rows=P, func=ACT.Copy, **kw):
                act.wait_ge(S["mm"], at("mm", step, b))
                nc.scalar.activation(dst, bank[0:rows, banks[0]:banks[1] + 1, :].rearrange("p h t -> p (h t)"),
                                     func, **kw).then_inc(S["ev"], note("ev", step))

            def take_gate(b, j):
                for h in range(2):
                    take(b, ("z", 1, j, h), gate[1][:, j, halves(h)], h, func=ACT.Silu)

            def tail(b, l):
                if l == 1:
                    take_gate(b, 0)
                take_pair(b, ("mu", l), mu[:, :], WORK)
                if l == 1:
                    take_gate(b, 1)
                    take_gate(b, 2)
                for j in range(J):
                    act.wait_ge(S["cen"], at("cen", (l, j), b))
                    nc.scalar.activation(sq[:, j, :], y[:, j, :], ACT.Square).then_inc(S["sq"], note("sq", (l, j)))
                take_pair(b, ("var", l), rs[:, :], WORK, func=ACT.Ln, bias=1e-5)
                act.wait_ge(S["ev"], at("ev", ("var", l), b))
                nc.scalar.activation(rs[:, :], rs[:, :], ACT.Exp, scale=-0.5).then_inc(S["rs"], note("rs", l))
                for j in range(J):
                    act.wait_ge(S["nrm"], at("nrm", (l, j), b))
                    nc.scalar.activation(y[:, j, :], y[:, j, :], ACT.Identity, scale=lnw[:, l, j:j + 1],
                                         bias=lnb[:, l, j:j + 1]).then_inc(S["aff"], note("aff", (l, j)))
                for c, banks in ((0, WORK), (1, SPARE)):
                    take_pair(b, ("out", l, c), o2[:, c, :], banks, rows=CH)

            act.wait_ge(loaded, 16 * LOADS)
            nc.scalar.activation(a0[:, :], a0[:, :], ACT.Exp).then_inc(exp_a, 1)
            nc.scalar.activation(a1[:, :], a1[:, :], ACT.Exp).then_inc(exp_a, 1)
            act.wait_ge(setup, 6)
            with act.Fori(0, NB) as b:
                front(b, 0)
                scans0(b)
                tail(b, 0)
                front(b, 1)
                scans1(b)
                tail(b, 1)

        @block.gpsimd
        def _(pool):
            def prepare_dt(b, l, i, j):
                delta = delta0[:, i % 2, j, :] if l == 0 else delta1[:, j, :]
                pool.wait_ge(S["dl"], at("dl", (l, i, j), b))
                if l == 1:
                    pool.wait_ge(S["yinit"], at("yinit", (1, j), b))
                    nc.gpsimd.tensor_tensor(du1[:, j, :], delta, u[:, j, :], ALU.mult).then_inc(S["du"], note("du", (1, 0, j)))
                    return
                for d, dt, src in zip(stored(du0[:, i % 2, j, :]), stored(delta), lines(u[:, j, :], SCANS[i][1])):
                    nc.gpsimd.tensor_tensor(d, dt, src, ALU.mult).then_inc(S["du"], note("du", (0, i, j)))

            def pair0(b, i, it, first, end):
                for p in range(2):
                    G = b * (K * N) + i * N + it * 2 + p
                    GS = b * NB_SPREAD + i * N + it * 2 + p
                    for j in range(J):
                        if first and p == 0:
                            pool.wait_ge(S["du"], at("du", (0, i, j), b))
                        if not (i == 0 and first):
                            pool.wait_ge(scanned[j], G - 1)
                        if j == 0:
                            pool.wait_ge(B_ready, GS + 1)
                        nc.gpsimd.tensor_tensor(source0[:, p, j, :], du0[:, i % 2, j, :], B_all[:, p, :],
                                                ALU.mult).then_inc(source_ready[j], 1)
                    if end and p == 0 and i < K - 1:
                        prepare_dt(b, 0, i + 1, 0)

            def scans0(b):
                for j in range(J):
                    prepare_dt(b, 0, 0, j)
                for i in range(K):
                    for lo, hi in PIECES:
                        if hi - lo == 1:
                            pair0(b, i, lo, lo == 0, hi == PAIRS)
                        else:
                            with pool.Fori(lo, hi) as it:
                                pair0(b, i, it, False, False)
                    if i < K - 1:
                        prepare_dt(b, 0, i + 1, 1)
                        prepare_dt(b, 0, i + 1, 2)

            def quad1(b, j, it, first, end):
                for m in range(4):
                    p = m % 2
                    G = b * (J * N) + j * N + it * 4 + m
                    GS = b * NB_SPREAD + (K * N + j * N) + it * 4 + m
                    if first and m == 0:
                        pool.wait_ge(S["du"], at("du", (1, 0, j), b))
                    if not (j == 0 and first and m < 2):
                        pool.wait_ge(dve1_ready, G - 1)
                        pool.wait_ge(pool1_ready, G * 3 - 3)
                    pool.wait_ge(B_ready, GS + 1)
                    nc.gpsimd.tensor_tensor(src1[:, p, :], du1[:, j, :], B_all[:, p, :],
                                            ALU.mult).then_inc(src1_ready, 1)
                    pool.wait_ge(src1_ready, G + 1)
                    for q in (0, 1, 3):
                        pool.wait_ge(gate1_ready, G * 4 + (q + 1))
                        state, src = state1[:, p, q, :], src1[:, p, :]
                        if q == 3:
                            state = state.rearrange("p (c r) -> p c r", c=SIDE)
                            src = src.rearrange("p (r c) -> p c r", r=SIDE)
                        nc.gpsimd.tensor_tensor(state, state, src, ALU.mult).then_inc(pool1_ready, 1)

            def scans1(b):
                for j in range(J):
                    prepare_dt(b, 1, 0, j)
                for j in range(J):
                    quad1(b, j, 0, True, False)
                    with pool.Fori(1, QUADS - 1) as it:
                        quad1(b, j, it, False, False)
                    quad1(b, j, QUADS - 1, False, True)

            def make_taps(l):
                nc.gpsimd.tensor_tensor(
                    taps[:, :, :], identity[:, :].unsqueeze(1).broadcast_to([P, 9, P]),
                    cw[:, l, J - 1, :].unsqueeze(2).broadcast_to([P, 9, P]), ALU.mult).then_inc(taps_ready, 1)

            pool.wait_ge(loaded, 16 * LOADS)
            make_taps(0)
            with pool.Fori(0, NB) as b:
                scans0(b)
                pool.wait_ge(S["yev"], at("yev", (0, K - 1, J - 1), b))
                make_taps(1)
                scans1(b)
                pool.wait_ge(S["yev"], at("yev", (1, J - 1), b))
                make_taps(0)

        @block.vector
        def _(dve):
            def front(b, l):
                if l == 0:
                    dve.wait_ge(load_x_done, b * 16 + 16)
                else:
                    dve.wait_ge(S["res"], at("res", (0, 1), b))
                for c in range(2):
                    for h in range(2):
                        nc.vector.bn_stats(stats[:, c, h, :], xT[:, c, halves(h)]).then_inc(
                            S["stat"], note("stat", (l, "bn")))
                dve.wait_ge(S["stat"], at("stat", (l, "bn"), b))
                nc.vector.memset(sq2[:, :], 0.0).then_inc(S["stat"], note("stat", (l, "carrier")))
                for c in range(2):
                    nc.vector.bn_aggr(mv[:, c, :], stats[:, c, :, :]).then_inc(S["stat"], note("stat", (l, "mv")))
                dve.wait_ge(S["stat"], at("stat", (l, "mv"), b))
                nc.vector.tensor_tensor(sq2[:, :], mv[:, :, 0], mv[:, :, 0], ALU.mult).then_inc(
                    S["stat"], note("stat", (l, "m2")))
                dve.wait_ge(S["stat"], at("stat", (l, "m2"), b))
                nc.vector.tensor_tensor(mv[:, :, 1], mv[:, :, 1], sq2[:, :], ALU.add).then_inc(
                    S["stat"], note("stat", (l, "msq")))
                dve.wait_ge(S["ev"], at("ev", ("gn", l), b))
                dve.wait_ge(S["stat"], at("stat", (l, "msq"), b))
                nc.vector.tensor_tensor(sq2[:, :], gs[:, :, 0], gs[:, :, 0], ALU.mult).then_inc(
                    S["stat"], note("stat", (l, "gm2")))
                dve.wait_ge(S["stat"], at("stat", (l, "gm2"), b))
                nc.vector.tensor_tensor(gvar[:, :], gs[:, :, 1], sq2[:, :], ALU.subtract).then_inc(
                    S["stat"], note("stat", (l, "gvar")))
                dve.wait_ge(S["gs"], at("gs", (l, "rstd"), b))
                for c in range(2):
                    nc.vector.tensor_scalar(xn[:, c, :], xT[:, c, :], gs[:, c, 0:1], rstd[:, c:c + 1],
                                            ALU.subtract, ALU.mult).then_inc(S["xn"], note("xn", (l, c)))
                for border in (padded[:, :, 0, :], padded[:, :, PAD - 1, :],
                               padded[:, :, 1:PAD - 1, 0], padded[:, :, 1:PAD - 1, PAD - 1]):
                    nc.vector.memset(border, 0.0).then_inc(S["pad"], note("pad", l))
                for tap in range(9):
                    dr, dc = tap // 3, tap % 3
                    for j in range(J - 1):
                        dst = u[:, j, :].rearrange("p (r c) -> p r c", c=SIDE)
                        src = padded[:, j, dr:dr + SIDE, dc:dc + SIDE]
                        if tap == 0:
                            dve.wait_ge(S["pad"], at("pad", l, b))
                            dve.wait_ge(S["ev"], at("ev", ("in", l, j, 1), b))
                            ins = nc.vector.tensor_scalar(dst, src, cw[:, l, j, 0:1], cb[:, l, j:j + 1],
                                                          ALU.mult, ALU.add)
                        else:
                            dve.wait_ge(S["conv"], at("conv", (l, j, tap - 1), b))
                            ins = nc.vector.scalar_tensor_tensor(dst, src, cw[:, l, j, tap:tap + 1], dst,
                                                                 ALU.mult, ALU.add)
                        ins.then_inc(S["conv"], note("conv", (l, j, tap)))

            def first_rest(b, l, i):
                slot = parts[:, i % 2, :]
                dve.wait_ge(S["p1"], at("p1", (l, i), b))
                nc.vector.tensor_tensor(xdbl[0:XR, :], xdbl[0:XR, :], slot[:, :], ALU.subtract).then_inc(
                    S["r1"], note("r1", (l, i)))

            def third_part(b, l, i):
                slot = parts[:, i % 2, :]
                dve.wait_ge(S["p2"], at("p2", (l, i), b))
                dve.wait_ge(S["r1"], at("r1", (l, i), b))
                nc.vector.tensor_tensor(slot[64:96, :], xdbl[64:96, :], slot[64:96, :], ALU.subtract).then_inc(
                    S["parts"], note("parts", (l, i)))

            def prepare_dt(b, l, i, j):
                delta = delta0[:, i % 2, j, :] if l == 0 else delta1[:, j, :]
                e = du0[:, i % 2, j, :] if l == 0 else e1[:, j, :]
                log_w, d = soft[l][:, j, :], soft[l][:, J, :]
                if j > 0 or i > 0:
                    dve.wait_ge(S["g1"], at("g1", (l, i, j - 1) if j > 0 else (l, i - 1, J - 1), b))
                dve.wait_ge(S["ln"], at("ln", (l, i, j), b))
                nc.vector.tensor_scalar(d, e, 1.0, 1.0, ALU.add, ALU.subtract).then_inc(S["d"], note("d", (l, i, j)))
                dve.wait_ge(S["d"], at("d", (l, i, j), b))
                nc.vector.tensor_tensor(e, e, d, ALU.subtract).then_inc(S["g1"], note("g1", (l, i, j)))
                dve.wait_ge(S["g1"], at("g1", (l, i, j), b))
                nc.vector.tensor_tensor(e, e, log_w, ALU.add).then_inc(S["g"], note("g", (l, i, j)))
                dve.wait_ge(S["g"], at("g", (l, i, j), b))
                nc.vector.scalar_tensor_tensor(delta, delta, 0.0, e, ALU.max, ALU.add).then_inc(
                    S["dl"], note("dl", (l, i, j)))

            def norm_again(b, l):
                for c in range(2):
                    nc.vector.tensor_scalar(xz[l][:, c, :], xT[:, c, :], gs[:, c, 0:1], rstd[:, c:c + 1],
                                            ALU.subtract, ALU.mult).then_inc(S["xz"], note("xz", (l, c)))

            def prepare_first(b, l):
                for j in range(J):
                    if j < J - 1:
                        dve.wait_ge(S["u"], at("u", (l, j), b))
                    else:
                        dve.wait_ge(S["ev"], at("ev", ("conv", l, 1), b))
                    nc.vector.tensor_scalar(y[:, j, :], u[:, j, :], skip[:, l, j:j + 1], None,
                                            ALU.mult).then_inc(S["yinit"], note("yinit", (l, j)))
                first_rest(b, l, 0)
                for j in range(J):
                    delta = delta0[:, 0, j, :] if l == 0 else delta1[:, j, :]
                    e = du0[:, 0, j, :] if l == 0 else e1[:, j, :]
                    dve.wait_ge(S["ev"], at("ev", ("dt", l, 0, j, 1), b))
                    nc.vector.scalar_tensor_tensor(e, delta, -1.0, delta, ALU.mult, ALU.max).then_inc(
                        S["ab_first"], note("ab_first", (l, j)))
                prepare_dt(b, l, 0, 0)
                third_part(b, l, 0)
                prepare_dt(b, l, 0, 1)
                prepare_dt(b, l, 0, 2)

            def step(b, i, n):
                if i == K - 1:
                    if n == 0:
                        norm_again(b, 0)
                    return
                if n == 1:
                    first_rest(b, 0, i + 1)
                if n == 9:
                    third_part(b, 0, i + 1)
                if n == 13:
                    prepare_dt(b, 0, i + 1, 0)
                if n == 14:
                    prepare_dt(b, 0, i + 1, 1)
                    prepare_dt(b, 0, i + 1, 2)

            def pair0(b, i, it, first):
                back = SCANS[i][2]
                for p in range(2):
                    G = b * (K * N) + i * N + it * 2 + p
                    GS = b * NB_SPREAD + i * N + it * 2 + p

                    def run(ap):
                        return ap[:, ::-1] if back else ap

                    def scan(j):
                        dve.wait_ge(decay_ready[j], G + 1)
                        dve.wait_ge(source_ready[j], G + 1)
                        if not (i == 0 and first):
                            dve.wait_ge(summed[j], G - 1)
                        nc.vector.tensor_tensor_scan(run(state0[:, p, j, :]), run(decay0[:, p, j, :]),
                                                     run(source0[:, p, j, :]), 0.0, ALU.mult, ALU.add).then_inc(scanned[j], 1)

                    def weigh(j):
                        dve.wait_ge(scanned[j], G + 1)
                        if j == 0:
                            dve.wait_ge(C_ready, GS + 1)
                        state = state0[:, p, j, :]
                        nc.vector.tensor_tensor(state, state, C_all[:, p, :], ALU.mult).then_inc(weighted[j], 1)

                    scan(0)
                    scan(1)
                    weigh(0)
                    scan(2)
                    weigh(1)
                    weigh(2)
                    if first and p == 0 and i > 0 and closes(i - 1):
                        collect0(b, i - 1)
                    if isinstance(it, int):
                        step(b, i, it * 2 + p)

            def collect0(b, i):
                for j in range(J):
                    dve.wait_ge(summed[j], b * (K * N) + (i + 1) * N)
                    if i < 2:
                        dve.wait_ge(S["yinit"], at("yinit", (0, j), b))
                    else:
                        before = max(q for q in range(i) if closes(q))
                        dve.wait_ge(S["yev"], at("yev", (0, before, j), b))
                    acc = yacc0[:, j, :, :].rearrange("p h t -> p (h t)")
                    for dst, src in zip(lines(y[:, j, :], SCANS[i][1]), stored(acc)):
                        nc.vector.tensor_tensor(dst, dst, src, ALU.add).then_inc(S["yev"], note("yev", (0, i, j)))

            def scans0(b):
                prepare_first(b, 0)
                for i in range(K):
                    for lo, hi in PIECES:
                        if hi - lo == 1:
                            pair0(b, i, lo, lo == 0)
                        else:
                            with dve.Fori(lo, hi) as it:
                                pair0(b, i, it, False)
                collect0(b, K - 1)

            def weigh1(b, j, G, GS, slot, start):
                dve.wait_ge(hsum_ready, G * 4)
                dve.wait_ge(C_ready, GS)
                if not start:
                    dve.wait_ge(summed1, G - 1)
                nc.vector.tensor_tensor(yc1[:, slot, :], hsum[:, slot, :, :].rearrange("p h t -> p (h t)"),
                                        C_all[:, slot, :], ALU.mult).then_inc(weighted1, 1)

            def quad1(b, j, it, first, end):
                for m in range(4):
                    p = m % 2
                    G = b * (J * N) + j * N + it * 4 + m
                    GS = b * NB_SPREAD + (K * N + j * N) + it * 4 + m

                    def scan(q):
                        dve.wait_ge(decay1_ready, G * 2 + (1 + q // 2))
                        state, decay = state1[:, p, q, :], decay1[m][q // 2]
                        if q % 2:
                            state, decay = state[:, ::-1], decay[:, ::-1]
                        nc.vector.tensor_tensor_scan(state, decay, state, 0.0, ALU.mult, ALU.add).then_inc(scanned1, 1)

                    dve.wait_ge(pool1_ready, G * 3 + 1)
                    scan(0)
                    dve.wait_ge(pool1_ready, G * 3 + 2)
                    scan(1)
                    dve.wait_ge(gate1_ready, G * 4 + 3)
                    dve.wait_ge(src1_ready, G + 1)
                    state = state1[:, p, 2, :].rearrange("p (c r) -> p c r", c=SIDE)
                    nc.vector.tensor_tensor(state, state, src1[:, p, :].rearrange("p (r c) -> p c r", r=SIDE),
                                            ALU.mult).then_inc(dve1_ready, 1)
                    if not (first and m == 0):
                        weigh1(b, j, G, GS, 1 - p, j == 0 and first and m == 1)
                    dve.wait_ge(dve1_ready, G + 1)
                    scan(2)
                    dve.wait_ge(pool1_ready, G * 3 + 3)
                    scan(3)

            def sums_of_steps(b, j):
                dve.wait_ge(S["dl"], at("dl", (1, 0, J - 1 if j == 1 else j), b))
                if j > 0:
                    dve.wait_ge(S["cs"], at("cs", (j - 1, Q - 1), b))
                nc.vector.tensor_copy(delta_cols.rearrange("p (c r) -> p c r", c=SIDE),
                                      delta1[:, j, :].rearrange("p (r c) -> p c r", r=SIDE)).then_inc(
                    S["dc"], note("dc", j))
                dve.wait_ge(S["dc"], at("dc", j, b))
                for q in range(Q):
                    src, dst = delta1[:, j, :] if q < 2 else delta_cols, csum[j % 2][:, q, :]
                    if q % 2:
                        src, dst = src[:, ::-1], dst[:, ::-1]
                    nc.vector.tensor_tensor_scan(dst, one[:, :].broadcast_to([P, T]), src, 0.0,
                                                 ALU.mult, ALU.add).then_inc(S["cs"], note("cs", (j, q)))

            def scans1(b):
                prepare_first(b, 1)
                sums_of_steps(b, 0)
                for j in range(J):
                    quad1(b, j, 0, True, False)
                    with dve.Fori(1, QUADS - 1) as it:
                        quad1(b, j, it, False, False)
                    if j < J - 1:
                        sums_of_steps(b, j + 1)
                    else:
                        norm_again(b, 1)
                    quad1(b, j, QUADS - 1, False, True)
                    G = b * (J * N) + (j + 1) * N
                    weigh1(b, j, G, b * NB_SPREAD + (K * N + (j + 1) * N), 1, False)
                    dve.wait_ge(summed1, G)
                    dve.wait_ge(S["yinit"], at("yinit", (1, j), b))
                    nc.vector.tensor_tensor(y[:, j, :], y[:, j, :], yacc1[:, :, :].rearrange("p h t -> p (h t)"),
                                            ALU.add).then_inc(S["yev"], note("yev", (1, j)))

            def tail(b, l):
                dve.wait_ge(S["ev"], at("ev", ("mu", l), b))
                for j in range(J):
                    nc.vector.tensor_tensor(y[:, j, :], y[:, j, :], mu[:, :], ALU.subtract).then_inc(
                        S["cen"], note("cen", (l, j)))
                dve.wait_ge(S["rs"], at("rs", l, b))
                for j in range(J):
                    nc.vector.tensor_tensor(y[:, j, :], y[:, j, :], rs[:, :], ALU.mult).then_inc(
                        S["nrm"], note("nrm", (l, j)))
                for j in range(J):
                    dve.wait_ge(S["aff"], at("aff", (l, j), b))
                    if l == 0:
                        dve.wait_ge(S["silu"], at("silu", (0, j), b))
                    elif j == 0:
                        dve.wait_ge(S["ev"], at("ev", ("z", 1, J - 1, 1), b))
                    nc.vector.tensor_tensor(y[:, j, :], y[:, j, :], gate[l][:, j, :], ALU.mult).then_inc(
                        S["gat"], note("gat", (l, j)))
                for c in range(2):
                    dve.wait_ge(S["ev"], at("ev", ("out", l, c), b))
                    nc.vector.tensor_tensor(xT[:, c, :], xT[:, c, :], o2[:, c, :], ALU.add).then_inc(
                        S["res"], note("res", (l, c)))

            dve.wait_ge(loaded, 16 * LOADS)
            nc.vector.memset(one[:, :], 1.0).then_inc(setup, 1)
            nc.vector.tensor_copy(pick_row[:, :], pick_f[:, :]).then_inc(setup, 1)
            nc.vector.tensor_reduce(skip[:, 0, :], dk[:, :, :], mybir.AxisListType.X, ALU.add).then_inc(setup, 1)
            nc.vector.tensor_scalar(skip[:, 1, :], skip[:, 1, :], float(Q), None, ALU.mult).then_inc(setup, 1)
            dve.wait_ge(exp_a, 2)
            nc.vector.tensor_scalar(a0[:, :], a0[:, :], -1.0, None, ALU.mult).then_inc(setup, 1)
            nc.vector.tensor_scalar(a1[:, :], a1[:, :], -1.0, None, ALU.mult).then_inc(setup, 1)
            dve.wait_ge(setup, 6)
            with dve.Fori(0, NB) as b:
                front(b, 0)
                scans0(b)
                tail(b, 0)
                front(b, 1)
                scans1(b)
                tail(b, 1)


def kernel(**inputs):
    import numpy as np
    import concourse.bacc as bacc
    from concourse.bass_utils import run_bass_kernel_spmd

    v = {k: np.asarray(a) for k, a in inputs.items()}
    L0, L1 = "L0_conv_", "L1_conv_"

    def channels(a):
        return np.moveaxis(a.reshape(J, P, *a.shape[1:]), 0, 1)

    def three(w):
        return channels(np.concatenate([w[:, R:]] * 3 + [w[:, :R]], axis=1))

    group = np.zeros((CH, CH), np.float32)
    size = C // 32
    for g in range(CH // size):
        group[g * size:(g + 1) * size, g * size:(g + 1) * size] = 1.0 / size
    arrays = {
        "x": v["x"].reshape(-1, T, C).transpose(0, 2, 1),
        "w_in": np.stack([v[L0 + "W_in"].T, v[L1 + "W_in"]]),
        "conv_w": np.stack([channels(v[l + "conv_w"].reshape(DI, 9)) for l in (L0, L1)], axis=1),
        "conv_b": np.stack([channels(v[l + "conv_b"]) for l in (L0, L1)], axis=1),
        "w_x0": np.stack([three(v[L0 + "x_proj_weight"][k].T) for k in range(K)]),
        "w_dt0": v[L0 + "dt_projs_weight"].transpose(0, 2, 1),
        "dt_b0": np.stack([channels(v[L0 + "dt_projs_bias"][k]) for k in range(K)], axis=1),
        "a_log0": v[L0 + "A_logs"].reshape(K, J, P, N).transpose(2, 0, 1, 3).reshape(P, K * J * N),
        "d0": v[L0 + "Ds"].reshape(K, J, P).transpose(2, 1, 0),
        "w_x1": three(v[L1 + "W_x"]),
        "w_dt1": v[L1 + "W_dt"],
        "dt_b1": channels(v[L1 + "b_dt"]),
        "a_log1": channels(v[L1 + "A_log"]).reshape(P, J * N),
        "d1": channels(v[L1 + "D_param"]),
        "ln_w": np.stack([channels(v[L0 + "ln_w"]), channels(v[L1 + "gamma"])], axis=1),
        "ln_b": np.stack([channels(v[L0 + "ln_b"]), channels(v[L1 + "beta"])], axis=1),
        "w_out": np.stack([v[L0 + "W_out"].T, v[L1 + "W_out"]]),
        "group_mean": group,
        "eye": np.eye(P, dtype=np.float32),
        "pick": np.tile(np.eye(2 * N, dtype=np.float32), (3, 1)),
        "mean_one": np.full((P, P), 1.0 / DI, np.float32),
    }
    arrays = {k: np.ascontiguousarray(a) for k, a in arrays.items()}

    def build(counts):
        nc = bacc.Bacc("TRN2", target_bir_lowering=False, num_devices=1)
        ins = {k: nc.dram_tensor("in_" + k, a.shape, mybir.dt.from_np(a.dtype), kind="ExternalInput").ap()
               for k, a in arrays.items()}
        out = nc.dram_tensor("out_x", arrays["x"].shape, F32, kind="ExternalOutput").ap()
        program(nc, counts, out=out, **ins)
        return nc

    first = Counts()
    build(first)
    nc = build(Counts(first))
    r = run_bass_kernel_spmd(nc, [{"in_" + k: a for k, a in arrays.items()}], core_ids=[0])
    y = np.asarray(r.results[0]["out_x"])
    return np.ascontiguousarray(y.transpose(0, 2, 1)).reshape(v["x"].shape)
```
